# Optimizing a Trainium2 kernel written in Bass

```python
import numpy as np
import jax
import jax.numpy as jnp

def _softmax(x, axis=-1):
    return jax.nn.softmax(x, axis=axis)

def _gelu(x):
    return jax.nn.gelu(x, approximate=True)

def _silu(x):
    return jax.nn.silu(x)

def _sigmoid(x):
    return jax.nn.sigmoid(x)

def _layernorm(x, axis=-1, eps=1e-05):
    m = jnp.mean(x, axis=axis, keepdims=True)
    v = jnp.var(x, axis=axis, keepdims=True)
    return (x - m) / jnp.sqrt(v + eps)

def _scatter_add(tgt, idx, src, axis=0):
    return tgt.at[idx].add(src)

def _segment_sum(src, seg, n):
    return jax.ops.segment_sum(src, seg, n)
kernel_name = 'mk_gnn_resnorm_d1_gnn_r8_3df9fb'

def setup_inputs(seed: int=0):
    np.random.seed(seed)
    _w = jnp.asarray

    def _rec_inputs():
        import jax
        import jax.numpy as jnp
        _gk = jax.random.key(seed)
        x = -0.0006008 + 1.001 * jax.random.normal(jax.random.fold_in(_gk, 1), (6250, 128), jnp.float32)
        src = jax.random.randint(jax.random.fold_in(_gk, 2), (100000,), 0, 6250, jnp.int32)
        dst = jax.random.randint(jax.random.fold_in(_gk, 3), (100000,), 0, 6250, jnp.int32)
        _o = jnp.argsort(dst, stable=True)
        src = src[_o]
        dst = dst[_o]
        edge_attr_128 = 0.000167468 + 1.0002 * jax.random.normal(jax.random.fold_in(_gk, 11), (100000, 128), jnp.float32)
        return (x, src, dst, edge_attr_128)
    x, src, dst, edge_attr_128 = _rec_inputs()

    def _L0_gnn_setup():
        import jax, jax.numpy as jnp
        import numpy as np
        N_NODES = 2500
        N_EDGES = 40000
        D = 128
        LN_EPS = 1e-05
        key = jax.random.key(seed)
        k1, k2, k3, k4 = jax.random.split(key, 4)
        x = jax.random.normal(k1, (N_NODES, D), dtype=jnp.float32)
        edge_index = jax.random.randint(k2, (2, N_EDGES), 0, N_NODES, dtype=jnp.int64)
        edge_attr = jax.random.normal(k3, (N_EDGES, D), dtype=jnp.float32)
        W = jax.random.normal(k4, (3 * D, D), dtype=jnp.float32) / np.sqrt(3 * D)
        b = jnp.zeros((D,), dtype=jnp.float32)
        gamma = jnp.ones((D,), dtype=jnp.float32)
        beta = jnp.zeros((D,), dtype=jnp.float32)
        return {'x': x, 'edge_index': edge_index, 'edge_attr': edge_attr, 'W': W, 'b': b, 'gamma': gamma, 'beta': beta}
    _L0_gnn_all = _L0_gnn_setup()
    _L0_gnn_in = {k: v for k, v in _L0_gnn_all.items() if k in ('W', 'b', 'gamma', 'beta')}
    del _L0_gnn_all
    return {'x': x, 'src': src, 'dst': dst, 'edge_attr_128': edge_attr_128, 'L0_gnn_W': _L0_gnn_in['W'], 'L0_gnn_b': _L0_gnn_in['b'], 'L0_gnn_gamma': _L0_gnn_in['gamma'], 'L0_gnn_beta': _L0_gnn_in['beta']}

def reference(x, src, dst, edge_attr_128, L0_gnn_W, L0_gnn_b, L0_gnn_gamma, L0_gnn_beta):
    import jax
    import jax.numpy as jnp

    def _L0_gnn_ref(x, edge_index, edge_attr, W, b, gamma, beta):
        import jax, jax.numpy as jnp
        import numpy as np
        N_NODES = 2500
        N_EDGES = 40000
        D = 128
        LN_EPS = 1e-05
        row, col = (edge_index[0], edge_index[1])
        msg_in = jnp.concatenate([x[row], x[col], edge_attr], axis=-1)
        h = msg_in @ W + b
        mu = jnp.mean(h, axis=-1, keepdims=True)
        var = jnp.mean(jnp.square(h - mu), axis=-1, keepdims=True)
        h = (h - mu) * jax.lax.rsqrt(var + LN_EPS) * gamma + beta
        msg = jax.nn.relu(h)
        out = jax.ops.segment_sum(msg, row, num_segments=x.shape[0])
        return out
    edge_index = jnp.stack([src, dst])
    x = _layernorm(x + _L0_gnn_ref(x, edge_index, edge_attr_128, L0_gnn_W, L0_gnn_b, L0_gnn_gamma, L0_gnn_beta), axis=-1)
    return x

_drawn_inputs = setup_inputs


def setup_inputs(seed=0):
    import zlib

    import numpy as np

    out = dict(_drawn_inputs(seed))
    spreads = {'L0_gnn_b': (0.0, 0.1), 'L0_gnn_gamma': (1.0, 0.2), 'L0_gnn_beta': (0.0, 0.1)}
    factors = {}
    for name, (base, spread) in spreads.items():
        noise = np.random.default_rng([zlib.crc32(name.encode()), seed]).standard_normal(out[name].shape)
        drawn = base * np.exp(spread * noise) if base else spread * noise
        out[name] = jnp.asarray(drawn.astype(out[name].dtype))
    for name, factor in factors.items():
        out[name] = (out[name] * factor).astype(out[name].dtype)
    return out
```

```python
import concourse.bass as bass
from concourse import mybir
from contextlib import ExitStack

F32 = mybir.dt.float32
BF16 = mybir.dt.bfloat16
I32 = mybir.dt.int32
ALU = mybir.AluOpType
ACT = mybir.ActivationFunctionType
AX = mybir.AxisListType

P = 128
D = 128
LN_EPS = 1e-5
NG_COLS = 8
GE = P * NG_COLS
SUPER = 512
SJ = SUPER // P
ROW = D + 1
RING = 4


def bass_gnn_resnorm(nc, x, src, dst, edge, W, b, gamma, beta, out):
    N = x.shape[0]
    E = src.shape[0]
    NB = -(-N // P)
    N_LAST = N - (NB - 1) * P
    NG = -(-E // GE)
    OVER = NG * GE - E
    C = NG * NG_COLS
    BK = NB + 1
    NS = (E + NB * SUPER) // SUPER
    NS_ALL = NS + NB + 1
    assert OVER % NG_COLS == 0 and NG % 2 == 0 and E % GE != 0

    tabA = nc.dram_tensor("tabA", (NB * P, D), F32)
    tabB = nc.dram_tensor("tabB", (NB * P, D), F32)
    rows = nc.dram_tensor("rows", (NS_ALL * SUPER, ROW), F32)
    runs = nc.dram_tensor("runs", (NS * P, D), F32)
    rows_ap = rows.ap()
    rows_quads = rows_ap.rearrange("(r j) c -> r (j c)", j=SJ)
    rows_super = rows_ap.rearrange("(s p j) c -> s p (j c)", p=P, j=SJ)
    runs_super = runs.ap().rearrange("(s p) d -> s p d", p=P)
    tabA_v = tabA.ap().rearrange("(t p) d -> p t d", p=P)
    tabB_v = tabB.ap().rearrange("(t p) d -> p t d", p=P)
    x_v = x[0:(NB - 1) * P, :].rearrange("(t p) d -> p t d", p=P)
    out_v = out[0:(NB - 1) * P, :].rearrange("(t p) d -> p t d", p=P)
    edge_groups = edge[0:(NG - 1) * GE, :].rearrange("(g p j) d -> g p (j d)", p=P, j=NG_COLS)
    edge_last = edge[E - GE:E, :].rearrange("(p j) d -> p (j d)", j=NG_COLS)

    ctx = ExitStack()
    with ctx:
        def sb(name, shape, dt=F32):
            return ctx.enter_context(nc.sbuf_tensor(name, shape, dt))

        def sem(name):
            return ctx.enter_context(nc.semaphore(name))

        def sems(name, n):
            return [sem(f"{name}{i}") for i in range(n)]

        bank = [ctx.enter_context(nc.psum_tensor(f"bank{i}", [P, 512], F32)) for i in range(8)]

        iota_row = sb("iota_row", [P, P])
        iota_col = sb("iota_col", [P, 1])
        iota_sup = sb("iota_sup", [P, NS])
        ident = sb("ident", [P, P])
        before = sb("before", [P, P], BF16)
        not_before = sb("not_before", [P, P], BF16)
        ones_bf = sb("ones_bf", [P, P], BF16)
        ones_row = sb("ones_row", [1, P])
        eps128 = sb("eps128", [P, 1])
        w_sb = sb("w_sb", [P, 3, D])
        w_mean = sb("w_mean", [P, 3])
        wc = sb("wc", [P, 3, D])
        vecs = sb("vecs", [P, 3, D])
        b_mean = sb("b_mean", [P, 1])
        bc = sb("bc", [P, D])
        gamma_s = sb("gamma_s", [P, D])
        gb = vecs[:, 1, :]
        beta_bc = vecs[:, 2, :]
        idx_rows = sb("idx_rows", [NG, 2, GE], I32)
        idx_f = sb("idx_f", [NG, 2, GE])
        src_i = sb("src_i", [P, C], I32)
        dst_i = sb("dst_i", [P, C], I32)
        hi_i = sb("hi_i", [P, C], I32)
        lo_i = sb("lo_i", [P, C], I32)
        hi_bf = sb("hi_bf", [P, C], BF16)
        lo_f = sb("lo_f", [P, C])
        onehot = sb("onehot", [P, BK, C], BF16)
        tot = sb("tot", [P, BK, NG_COLS])
        cum = sb("cum", [P, BK * NG_COLS])
        excl = sb("excl", [P, BK, NG_COLS])
        cnt = sb("cnt", [P, BK])
        cnt_i = sb("cnt_i", [P, BK], I32)
        nsup = sb("nsup", [P, BK])
        sup_end = sb("sup_end", [P, BK])
        sup_start = sb("sup_start", [P, BK])
        shift = sb("shift", [P, BK])
        base = sb("base", [P, BK, NG_COLS])
        start_col = sb("start_col", [BK, 1])
        reached = sb("reached", [BK, NS])
        ones_f = sb("ones_f", [BK, P])
        blk = sb("blk", [P, NS])
        same = sb("same", [P, NS])
        blk_p = sb("blk_p", [P, NS])
        blk_idx = sb("blk_idx", [P, NS], I32)
        last_f = sb("last_f", [P, 2 * NB])
        last_idx = sb("last_idx", [P, 2 * NB], I32)
        fill = sb("fill", [P, SJ, ROW])
        xq = sb("xq", [P, 2, 4, D])
        x_last = sb("x_last", [P, D])
        xT = sb("xT", [P, 2, 512])
        a_st = sb("a_st", [P, 2, 4, D])
        b_st = sb("b_st", [P, 2, 4, D])
        e_sb = sb("e_sb", [P, RING, GE])
        eT = sb("eT", [P, 2, 512])
        b_rows = sb("b_rows", [P, RING, NG_COLS, D])
        stage = sb("stage", [P, RING, NG_COLS, ROW])
        prod = sb("prod", [P, BK, NG_COLS])
        pos_idx = sb("pos_idx", [P, RING, NG_COLS], I32)
        dst_idx = sb("dst_idx", [P, RING, NG_COLS], I32)
        hs = [stage[:, k, 0:SJ, :] for k in range(RING)]
        a_blk = [b_rows[:, k, 0, :] for k in range(RING)]
        quads = [e_sb[:, k // 2, 512 * (k % 2):512 * (k % 2) + 512] for k in range(2 * RING)]
        sel = [q.rearrange("p (j n) -> p j n", j=SJ) for q in quads[0:4]]
        selT = quads[4:6]
        pre = [q.rearrange("p (j n) -> p j n", j=SJ) for q in quads[6:8]]
        msg = [b_rows[:, k, SJ:2 * SJ, :] for k in range(2)]
        run = sb("run", [P, RING, D])
        blk_now = sb("blk_now", [P, RING], I32)
        ssq = sb("ssq", [P, 2, SJ])
        std = sb("std", [P, 2, SJ])
        rstd = sb("rstd", [P, 2, SJ])
        CH = 7
        NCH = NB // CH
        assert NCH * CH == NB
        y = onehot[:, 0:16, :].rearrange("p b c -> p (b c)").bitcast(F32)[:, 0:NB * D].rearrange("p (t d) -> p t d", t=NB)
        xr = onehot[:, 16:32, :].rearrange("p b c -> p (b c)").bitcast(F32)[:, 0:NB * D].rearrange("p (t d) -> p t d", t=NB)
        y2 = onehot[:, 32:48, :].rearrange("p b c -> p (b c)").bitcast(F32)[:, 0:NB * D].rearrange("p (t d) -> p t d", t=NB)
        ysum = sb("ysum", [P, NB])
        ymean = sb("ymean", [P, NB])
        yssq = sb("yssq", [P, NB])
        ystd = sb("ystd", [P, NB])
        yrstd = sb("yrstd", [P, NB])

        s_iota = sem("iota_made")
        s_const = sem("constants_made")
        s_idx_in = sem("indices_loaded")
        s_idx_f = sem("indices_as_float")
        s_idx_t = sem("indices_transposed")
        s_dve = sem("dve_chain")
        s_hot = sem("onehot_made")
        s_cnt = sem("counts_summed")
        s_base = sem("bases_made")
        s_col = sem("starts_transposed")
        s_reach = sem("starts_compared")
        s_blk = sem("blocks_summed")
        s_tabs = sem("index_tables_made")
        s_fillv = sem("fill_rows_made")
        s_fill = sem("fills_landed")
        s_w = sem("weights_loaded")
        s_wc = sem("weights_centred")
        s_xz = sem("last_block_cleared")
        s_x = sems("x_quad_loaded", 2)
        s_xl = sem("last_block_loaded")
        s_xt = sem("x_transposed")
        s_xc = sem("xT_copied")
        s_ab = sem("tables_multiplied")
        s_ac = sem("tables_copied")
        s_bb = sem("bias_added")
        s_tab = sems("tables_stored", 2)
        s_turn = sem("pool_turns")
        e_ready = sems("e_loaded", RING)
        e_used = sem("e_transposed")
        eT_ready = sem("eT_copied")
        h_done = sem("edges_multiplied")
        rank_mm = sem("ranks_summed")
        rank_read = sem("ranks_read")
        pos_ready = sem("positions_made")
        dsti_ready = sem("dst_indices_made")
        b_ready = sems("b_rows_gathered", RING)
        lo_ready = sem("node_numbers_staged")
        st_ready = sem("rows_staged")
        st_free = sems("rows_scattered", RING)
        hs_ready = sems("hs_loaded", RING)
        n_idx = sem("block_index_made")
        a_ready = sems("a_block_gathered", RING)
        n_sel = sem("selectors_made")
        n_selT = sem("selectors_transposed")
        n_selTc = sem("selT_copied")
        n_a = sem("a_rows_selected")
        n_pre = sem("pre_made")
        n_ssq = sem("squares_summed")
        n_std = sem("std_made")
        n_norm = sem("normalised")
        n_msg = sem("messages_made")
        n_o = sem("messages_summed")
        n_run = sem("runs_made")
        n_dve = sem("norm_chain")
        run_st = sems("run_stored", RING)
        n_rs = sem("rstd_made")
        s_a1 = sem("a_copied")
        tr_half = sem("e_first_half_transposed")
        f_x = sems("x_reloaded", NCH)
        f_g = sems("runs_gathered", NCH)
        f_dve = sem("final_chain")
        f_sq = sem("final_squared")
        f_ss = sem("final_sums")
        f_sd = sem("final_std")
        f_y = sem("final_rows")
        f_out = sem("output_stored")

        NQ = (NB - 1) // 4
        assert NQ * 4 == NB - 1 and NQ % 2 == 0
        NIT = NG // RING
        NIT2 = NS // RING
        LAST = NG - NIT * RING
        assert NS % RING == 0

        def load_edges(eng, g, k, u, first=False, last=False):
            if not first:
                eng.wait_ge(e_used, g - RING + 1)
            eng.dma_start(e_sb[:, k, :], edge_last if last else edge_groups[g]).then_inc(e_ready[k], 16)

        def load_super(eng, s, k, first=False):
            if not first:
                eng.wait_ge(n_pre, s - RING + 1)
            eng.dma_start(hs[k], rows_super[s]).then_inc(hs_ready[k], 16)

        def store_run(eng, s, k):
            eng.wait_ge(n_run, s + 1)
            eng.dma_start(runs_super[s], run[:, k, :]).then_inc(run_st[k], 16)

        block = ctx.enter_context(nc.Block())

        def group_trips(eng, step):
            for k in range(RING):
                step(k, k, 0, True)
            with eng.Fori(1, NIT) as i:
                for k in range(RING):
                    step(i * RING + k, k, i, False)
            for k in range(LAST):
                step(NIT * RING + k, k, NIT, False)

        def super_trips(eng, step):
            for n in range(-3, RING):
                step(n, n % RING, n // RING)
            with eng.Fori(1, NIT2 - 1) as i:
                for k in range(RING):
                    step(i * RING + k, k, i)
            for n in range(NS - RING, NS + 2):
                step(n, n % RING, n // RING)

        def inside(n, d):
            return not isinstance(n, int) or 0 <= n + d < NS

        def early(n, d, lim):
            return isinstance(n, int) and n + d < lim

        @block.sync
        def _(sp):
            for n, v in enumerate((src, dst)):
                whole = v[0:(NG - 2) * GE].rearrange("(g e) -> g e", e=GE)
                sp.dma_start(idx_rows[0:NG - 2, n, :], whole).then_inc(s_idx_in, 16)
                sp.dma_start(idx_rows[NG - 2:NG - 1, n, :], v[(NG - 2) * GE:(NG - 1) * GE].rearrange("(g e) -> g e", g=1)).then_inc(s_idx_in, 16)
                sp.dma_start(idx_rows[NG - 1:NG, n, :], v[E - GE:E].rearrange("(g e) -> g e", g=1)).then_inc(s_idx_in, 16)
            sp.dma_start(w_sb[:], W.rearrange("(t p) d -> p t d", p=P)).then_inc(s_w, 16)
            for n, v in enumerate((b, gamma, beta)):
                sp.dma_start(vecs[:, n, :], v.partition_broadcast(P)).then_inc(s_w, 16)

            def quad(q, k, first):
                if not first:
                    sp.wait_ge(s_xt, q - 1)
                sp.dma_start(xq[:, k, :, :], x_v[:, bass.ds(q * 4, 4), :]).then_inc(s_x[k], 16)

            def store(q, k):
                sp.wait_ge(s_ac, 2 * q + 2)
                sp.dma_start(tabA_v[:, bass.ds(q * 4, 4), :], a_st[:, k, :, :]).then_inc(s_tab[k], 16)
                sp.wait_ge(s_bb, q + 1)
                sp.dma_start(tabB_v[:, bass.ds(q * 4, 4), :], b_st[:, k, :, :]).then_inc(s_tab[k], 16)

            quad(0, 0, True)
            quad(1, 1, True)
            sp.wait_ge(s_xz, 1)
            sp.dma_start(x_last[0:N_LAST, :], x[(NB - 1) * P:N, :]).then_inc(s_xl, 16)
            for k in range(2):
                store(k, k)
                quad(k + 2, k, False)
            with sp.Fori(1, NQ // 2 - 1) as i:
                for k in range(2):
                    store(2 * i + k, k)
                    quad(2 * i + 2 + k, k, False)
            for k in range(2):
                store(NQ - 2 + k, k)
            sp.wait_ge(s_ac, 2 * NQ + 1)
            sp.dma_start(tabA_v[:, NB - 1, :], a_st[:, 0, 0, :]).then_inc(s_tab[0], 16)
            sp.wait_ge(s_bb, NQ + 1)
            sp.dma_start(tabB_v[:, NB - 1, :], b_st[:, 0, 0, :]).then_inc(s_tab[0], 16)

            for k in range(RING):
                load_edges(sp, k, k, 0, first=True)
            with sp.Fori(1, NIT) as i:
                for k in range(RING):
                    load_edges(sp, i * RING + k, k, i)
            for k in range(LAST):
                g = NIT * RING + k
                load_edges(sp, g, k, NIT, last=(g == NG - 1))

            for k in range(RING):
                sp.wait_ge(st_free[k], 16 * NG_COLS * (NIT + (k < LAST)))

            def step(n, k, i):
                if inside(n, 3):
                    load_super(sp, n + 3, (k + 3) % RING, first=early(n, 3, RING))
                if inside(n, -2):
                    store_run(sp, n - 2, (k - 2) % RING)
            super_trips(sp, step)

            for k in range(RING):
                sp.wait_ge(run_st[k], 16 * NIT2)
            sp.wait_ge(f_ss, 1)
            for c in range(NCH):
                lo, hi = c * CH, (c + 1) * CH
                if c < NCH - 1:
                    sp.dma_start(xr[:, lo:hi, :], x_v[:, lo:hi, :]).then_inc(f_x[c], 16)
                else:
                    sp.dma_start(xr[:, lo:hi - 1, :], x_v[:, lo:hi - 1, :]).then_inc(f_x[c], 16)
                    sp.dma_start(xr[0:N_LAST, hi - 1, :], x[(NB - 1) * P:N, :]).then_inc(f_x[c], 16)
            for c in range(NCH):
                lo, hi = c * CH, (c + 1) * CH
                sp.wait_ge(f_y, c + 1)
                if c < NCH - 1:
                    sp.dma_start(out_v[:, lo:hi, :], y[:, lo:hi, :]).then_inc(f_out, 16)
                else:
                    sp.dma_start(out_v[:, lo:hi - 1, :], y[:, lo:hi - 1, :]).then_inc(f_out, 16)
                    sp.dma_start(out[(NB - 1) * P:N, :], y[0:N_LAST, hi - 1, :]).then_inc(f_out, 16)
            sp.wait_ge(f_out, 16 * (NCH + 1))

        @block.gpsimd
        def _(pool):
            nc.gpsimd.iota(iota_row[:], [[1, P]], base=0, channel_multiplier=0,
                           allow_small_or_imprecise_dtypes=True).then_inc(s_iota, 1)
            nc.gpsimd.iota(iota_col[:], [[0, 1]], base=0, channel_multiplier=1,
                           allow_small_or_imprecise_dtypes=True).then_inc(s_iota, 1)
            nc.gpsimd.iota(iota_sup[:], [[1, NS]], base=0, channel_multiplier=0,
                           allow_small_or_imprecise_dtypes=True).then_inc(s_iota, 1)
            nc.gpsimd.memset(ones_bf[:], 1.0).then_inc(s_const, 1)
            nc.gpsimd.memset(ones_row[:], 1.0).then_inc(s_const, 1)
            nc.gpsimd.memset(ones_f[:], 1.0).then_inc(s_const, 1)
            nc.gpsimd.memset(eps128[:], D * LN_EPS).then_inc(s_const, 1)
            nc.gpsimd.memset(run[:], 0.0).then_inc(s_const, 1)
            nc.gpsimd.memset(x_last[:], 0.0).then_inc(s_xz, 1)
            nc.gpsimd.memset(fill[:], 0.0).then_inc(s_fillv, 1)
            pool.wait_ge(s_fillv, 1)
            nc.gpsimd.memset(fill[:, :, D:ROW], -1.0).then_inc(s_fillv, 1)

            pool.wait_ge(s_wc, 3)
            def bias(q, k, nblk=4):
                pool.wait_ge(s_ac, 2 * q + (2 if nblk == 4 else 1))
                nc.gpsimd.tensor_tensor(b_st[:, k, 0:nblk, :], b_st[:, k, 0:nblk, :],
                                        bc[:].unsqueeze(1).to_broadcast([P, nblk, D]), ALU.add).then_inc(s_bb, 1)
            with pool.Fori(0, NQ // 2) as i:
                for k in range(2):
                    bias(2 * i + k, k)
            bias(NQ, 0, 1)

            pool.wait_ge(s_fillv, 2)
            pool.wait_ge(s_tabs, 1)
            fill_rows = fill[:].rearrange("p j c -> p (j c)")
            for t in range(2 * NB):
                nc.gpsimd.indirect_dma_start(rows_quads, bass.IndirectOffsetOnAxis(last_idx[:, t:t + 1], 0),
                                             fill_rows, None).then_inc(s_fill, 16)

            pool.wait_ge(s_tab[0], 16 * (NQ + 2))
            pool.wait_ge(s_tab[1], 16 * NQ)

            def settle():
                pool.sem_inc(s_turn, 1)

            def gather_b(g, k, free):
                pool.wait_ge(dsti_ready, g + 1)
                if free:
                    pool.wait_ge(st_ready, 2 * (g - RING) + 2)
                settle()
                for j in range(NG_COLS):
                    nc.gpsimd.indirect_dma_start(b_rows[:, k, j, :], None, tabB.ap(),
                                                 bass.IndirectOffsetOnAxis(dst_idx[:, k, j:j + 1], 0)).then_inc(b_ready[k], 16)

            def scatter(g, k):
                pool.wait_ge(pos_ready, g + 1)
                pool.wait_ge(lo_ready, g + 1)
                pool.wait_ge(st_ready, 2 * g + 2)
                settle()
                for j in range(NG_COLS):
                    nc.gpsimd.indirect_dma_start(rows_ap, bass.IndirectOffsetOnAxis(pos_idx[:, k, j:j + 1], 0),
                                                 stage[:, k, j, :], None).then_inc(st_free[k], 16)

            gather_b(0, 0, False)
            gather_b(1, 1, False)
            pool.wait_ge(s_fill, 16 * 2 * NB)
            for k in range(RING):
                gather_b(k + 2, (k + 2) % RING, k + 2 >= RING)
                scatter(k, k)
            with pool.Fori(1, NIT) as i:
                for k in range(RING):
                    gather_b(i * RING + k + 2, (k + 2) % RING, True)
                    scatter(i * RING + k, k)
            for k in range(LAST):
                scatter(NIT * RING + k, k)

            def step(n, k, i):
                if inside(n, 2):
                    s, kk = n + 2, (k + 2) % RING
                    pool.wait_ge(n_idx, s + 1)
                    if not early(n, 2, RING):
                        pool.wait_ge(n_a, s - RING + 1)
                        settle()
                    nc.gpsimd.indirect_dma_start(a_blk[kk], None, tabA.ap(),
                                                 bass.IndirectOffsetOnAxis(blk_now[:, kk:kk + 1], 0)).then_inc(a_ready[kk], 16)
            super_trips(pool, step)

            for k in range(RING):
                pool.wait_ge(run_st[k], 16 * NIT2)
            for t in range(NB):
                nc.gpsimd.indirect_dma_start(y[:, t, :], None, runs.ap(),
                                             bass.IndirectOffsetOnAxis(last_idx[:, t:t + 1], 0)).then_inc(f_g[t // CH], 16)

        @block.tensor
        def _(pe):
            pe.wait_ge(s_const, 6)
            for v in range(2):
                pe.wait_ge(s_idx_f, v + 1)
                for j in range(NG_COLS):
                    o = bank[2 * v + j // 4][:, 0:4 * NG].rearrange("p (j g) -> p j g", j=4)
                    mm = pe.transpose(o[:, j % 4, :], idx_f[:, v, j::NG_COLS], ident[0:NG, 0:NG])
                mm.then_inc(s_idx_t, 1)

            pe.wait_ge(s_wc, 3)

            def quad(q, k, nblk=4, first=False):
                if nblk == 4:
                    pe.wait_ge(s_x[k], 16 * (q // 2 + 1) if isinstance(q, int) else 16 * (i2[0] + 1))
                else:
                    pe.wait_ge(s_xl, 16)
                if not first:
                    pe.wait_ge(s_xc, q - 1)
                for t in range(nblk):
                    mm = pe.transpose(bank[4 + k][:, t * P:(t + 1) * P], xq[:, k, t, :] if nblk == 4 else x_last[:], ident[:])
                mm.then_inc(s_xt, 1)
                pe.wait_ge(s_xc, q + 1)
                pe.wait_ge(s_ac, 2 * q) if not (isinstance(q, int) and q == 0) else None
                for t in range(nblk):
                    mm = pe.matmul(bank[6 + t // 2][:, (t % 2) * 256:(t % 2) * 256 + 256],
                                   xT[:, k, t * P:(t + 1) * P], wc[:, 0:2, :].rearrange("p t d -> p (t d)"),
                                   start=True, stop=True)
                mm.then_inc(s_ab, 1)

            i2 = [0]
            for k in range(2):
                quad(k, k, first=True)
            with pe.Fori(1, NQ // 2) as i:
                i2[0] = i
                for k in range(2):
                    quad(2 * i + k, k)
            quad(NQ, 0, 1)

            pe.wait_ge(s_hot, 1)

            def hot(g):
                return onehot[:, :, bass.ds(g * NG_COLS, NG_COLS)]

            total = bank[0][:, 0:BK * NG_COLS].rearrange("p (b j) -> p b j", j=NG_COLS)
            pe.matmul(total, ones_bf[:], hot(0), start=True, stop=False)
            with pe.Fori(1, NG - 1) as g:
                pe.matmul(total, ones_bf[:], hot(g), start=False, stop=False)
            pe.matmul(total, ones_bf[:], hot(NG - 1), start=False, stop=True).then_inc(s_cnt, 1)

            pe.wait_ge(s_base, 1)
            pe.transpose(bank[1][0:BK, 0:P], sup_start[:], ident[:]).then_inc(s_col, 1)
            pe.wait_ge(s_reach, 1)
            pe.matmul(bank[2][:, 0:NS], ones_f[0:NB, :], reached[0:NB, :], start=True, stop=True).then_inc(s_blk, 1)

            acc = bank[1][:, 0:BK * NG_COLS].rearrange("p (b j) -> p b j", j=NG_COLS)
            pe.matmul(bank[1][:, 0:BK * NG_COLS], ones_row[:], base[0:1, :, :].rearrange("p b j -> p (b j)"),
                      start=True, stop=False, skip_group_check=True)

            def step(g, k, u, first):
                if not (isinstance(g, int) and g == 0):
                    pe.wait_ge(rank_read, g)
                    pe.matmul(acc, not_before[:], hot(g - 1), start=False, stop=False, skip_group_check=True)
                pe.matmul(acc, before[:], hot(g), start=False, stop=True, skip_group_check=True).then_inc(rank_mm, 1)
                pe.wait_ge(e_ready[k], u * 16 + 16)
                for h in range(2):
                    if not (isinstance(g, int) and g == 0):
                        pe.wait_ge(eT_ready, 2 * g + h - 1)
                    for t in range(4):
                        j = 4 * h + t
                        mm = pe.transpose(bank[4 + h][:, t * P:(t + 1) * P], e_sb[:, k, j * D:(j + 1) * D], ident[:])
                    mm.then_inc(e_used, 1) if h else mm.then_inc(tr_half, 1)
                for h in range(2):
                    pe.wait_ge(eT_ready, 2 * g + h + 1)
                    if not (isinstance(g, int) and g == 0):
                        pe.wait_ge(st_ready, 2 * g + h - 1)
                    for t in range(4):
                        mm = pe.matmul(bank[6 + h][:, t * D:(t + 1) * D], eT[:, h, t * P:(t + 1) * P], wc[:, 2, :],
                                       start=True, stop=True)
                    mm.then_inc(h_done, 1)
            group_trips(pe, step)

            def step(n, k, i):
                if inside(n, 1):
                    s, b2 = n + 1, (k + 1) % 2
                    pe.wait_ge(n_sel, s + 1)
                    if not early(n, 1, 2):
                        pe.wait_ge(n_selTc, s - 1)
                    for j in range(SJ):
                        mm = pe.transpose(bank[b2][:, j * P:(j + 1) * P], sel[(k + 1) % RING][:, j, :], ident[:])
                    mm.then_inc(n_selT, 1)
                if inside(n, 0):
                    s, b2 = n, k % 2
                    pe.wait_ge(n_selTc, s + 1)
                    pe.wait_ge(a_ready[k], i * 16 + 16)
                    if not early(n, 0, 2):
                        pe.wait_ge(n_pre, s - 1)
                    for j in range(SJ):
                        mm = pe.matmul(bank[2 + b2][:, j * D:(j + 1) * D], selT[b2][:, j * P:(j + 1) * P], a_blk[k],
                                       start=True, stop=True)
                    mm.then_inc(n_a, 1)
                if inside(n, -1):
                    s, b2 = n - 1, (k + 1) % 2
                    pe.wait_ge(n_msg, s + 1)
                    if not early(n, -1, 2):
                        pe.wait_ge(n_run, s - 1)
                    for j in range(SJ):
                        mm = pe.matmul(bank[4 + b2][:, 0:D], sel[(k - 1) % RING][:, j, :], msg[b2][:, j, :],
                                       start=(j == 0), stop=(j == SJ - 1))
                    mm.then_inc(n_o, 1)
            super_trips(pe, step)

        @block.scalar
        def _(act):
            def quad(q, k, nblk=4, first=False):
                act.wait_ge(s_xt, q + 1)
                if not first:
                    act.wait_ge(s_ab, q - 1)
                nc.scalar.copy(xT[:, k, 0:nblk * P], bank[4 + k][:, 0:nblk * P]).then_inc(s_xc, 1)
                act.wait_ge(s_ab, q + 1)
                if not first:
                    act.wait_ge(s_tab[k], uses[0] * 32)
                if nblk == 1:
                    nc.scalar.copy(a_st[:, k, 0, :], bank[6][:, 0:D]).then_inc(s_a1, 1)
                    nc.scalar.copy(b_st[:, k, 0, :], bank[6][:, D:2 * D]).then_inc(s_ac, 1)
                    return
                for h in range(2):
                    o = bank[6 + h][:].rearrange("p (t w d) -> p t w d", t=2, w=2)
                    nc.scalar.copy(a_st[:, k, 2 * h:2 * h + 2, :], o[:, :, 0, :]).then_inc(s_a1, 1)
                    nc.scalar.copy(b_st[:, k, 2 * h:2 * h + 2, :], o[:, :, 1, :]).then_inc(s_ac, 1)
            uses = [0]
            for k in range(2):
                quad(k, k, first=True)
            with act.Fori(1, NQ // 2) as i:
                uses[0] = i
                for k in range(2):
                    quad(2 * i + k, k)
            uses[0] = NQ // 2
            quad(NQ, 0, 1)

            def step(g, k, u, first):
                if not first:
                    act.wait_ge(st_free[k], u * 16 * NG_COLS)
                act.wait_ge(s_tabs, 1)
                nc.scalar.copy(stage[:, k, :, D], lo_f[:, bass.ds(g * NG_COLS, NG_COLS)]).then_inc(lo_ready, 1)
                for h in range(2):
                    if h == 0:
                        act.wait_ge(tr_half, g + 1)
                    else:
                        act.wait_ge(e_used, g + 1)
                    if not (isinstance(g, int) and g == 0):
                        act.wait_ge(h_done, 2 * g + h - 1)
                    nc.scalar.copy(eT[:, h, :], bank[4 + h][:]).then_inc(eT_ready, 1)
            group_trips(act, step)

            def step(n, k, i):
                if inside(n, 1):
                    s, b2 = n + 1, (k + 1) % 2
                    act.wait_ge(n_selT, s + 1)
                    if not early(n, 1, 2):
                        act.wait_ge(n_a, s - 1)
                    nc.scalar.copy(selT[b2], bank[b2][:]).then_inc(n_selTc, 1)
                if inside(n, 0):
                    s, b2 = n, k % 2
                    act.wait_ge(n_pre, s + 1)
                    if not early(n, 0, 2):
                        act.wait_ge(n_std, s - 1)
                    for j in range(SJ):
                        a = nc.scalar.activation(eT[:, b2, j * D:(j + 1) * D], pre[b2][:, j, :], ACT.Square, accum_out=ssq[:, b2, j:j + 1])
                    a.then_inc(n_ssq, 1)
                    act.wait_ge(n_ssq, s + 1)
                    if not early(n, 0, 2):
                        act.wait_ge(n_rs, s - 1)
                    nc.scalar.activation(std[:, b2, :], ssq[:, b2, :], ACT.Sqrt, bias=eps128[:]).then_inc(n_std, 1)
                if inside(n, -1):
                    s, b2 = n - 1, (k + 1) % 2
                    act.wait_ge(n_norm, s + 1)
                    nc.scalar.activation(msg[b2], msg[b2], ACT.Relu).then_inc(n_msg, 1)
            super_trips(act, step)

            for c in range(NCH):
                lo, hi = c * CH, (c + 1) * CH
                act.wait_ge(f_dve, 3 * c + 3)
                nc.scalar.activation(y2[:, lo:hi, :], y[:, lo:hi, :], ACT.Square).then_inc(f_sq, 1)
                act.wait_ge(f_ss, c + 2)
                nc.scalar.activation(ystd[:, lo:hi], yssq[:, lo:hi], ACT.Sqrt, bias=eps128[:]).then_inc(f_sd, 1)


        @block.vector
        def _(dve):
            chain = [0]

            def link(ins):
                chain[0] += 1
                ins.then_inc(s_dve, 1)
                dve.wait_ge(s_dve, chain[0])

            dve.wait_ge(s_iota, 3)
            nc.vector.tensor_scalar(ident[:], iota_row[:], iota_col[:], None, ALU.is_equal).then_inc(s_const, 1)
            nc.vector.tensor_scalar(before[:], iota_row[:], iota_col[:], None, ALU.is_gt)
            nc.vector.tensor_scalar(not_before[:], iota_row[:], iota_col[:], None, ALU.is_le)
            for v in range(2):
                dve.wait_ge(s_idx_in, 96)
                nc.vector.tensor_copy(idx_f[:, v, :], idx_rows[:, v, :]).then_inc(s_idx_f, 1)
            dve.wait_ge(s_idx_t, 1)
            for h in range(2):
                o = src_i[:].rearrange("p (g j) -> p j g", j=NG_COLS)[:, 4 * h:4 * h + 4, :]
                a = nc.vector.tensor_copy(o, bank[h][:, 0:4 * NG].rearrange("p (j g) -> p j g", j=4))
            link(a)
            nc.vector.tensor_scalar(hi_i[:], src_i[:], 7, None, ALU.logical_shift_right)
            link(nc.vector.tensor_scalar(lo_i[:], src_i[:], P - 1, None, ALU.bitwise_and))
            link(nc.vector.tensor_copy(hi_bf[:], hi_i[:]))
            link(nc.vector.memset(hi_bf[0:OVER // NG_COLS, C - NG_COLS:C], float(NB)))
            for bk in range(BK):
                a = nc.vector.tensor_scalar(onehot[:, bk, :], hi_bf[:], float(bk), None, ALU.is_equal)
            a.then_inc(s_hot, 1)
            nc.vector.tensor_copy(lo_f[:], lo_i[:])
            dve.wait_ge(s_w, 64)
            link(nc.vector.tensor_reduce(w_mean[:], w_sb[:], AX.X, ALU.add))
            link(nc.vector.tensor_scalar(w_mean[:], w_mean[:], 1.0 / D, None, ALU.mult))
            nc.vector.tensor_tensor(wc[:], w_sb[:], w_mean[:].unsqueeze(2).to_broadcast([P, 3, D]), ALU.subtract).then_inc(s_wc, 1)
            link(nc.vector.tensor_reduce(b_mean[:], vecs[:, 0, :], AX.X, ALU.add))
            link(nc.vector.tensor_scalar(b_mean[:], b_mean[:], 1.0 / D, None, ALU.mult))
            nc.vector.tensor_scalar(bc[:], vecs[:, 0, :], b_mean[:], None, ALU.subtract).then_inc(s_wc, 1)
            nc.vector.tensor_scalar(gamma_s[:], gb, float(D) ** 0.5, None, ALU.mult).then_inc(s_wc, 1)
            dve.wait_ge(s_idx_t, 2)
            for h in range(2):
                o = dst_i[:].rearrange("p (g j) -> p j g", j=NG_COLS)[:, 4 * h:4 * h + 4, :]
                a = nc.vector.tensor_copy(o, bank[2 + h][:, 0:4 * NG].rearrange("p (j g) -> p j g", j=4))
            link(a)
            nc.vector.tensor_copy(dst_idx[:, 0, :], dst_i[:, 0:NG_COLS]).then_inc(dsti_ready, 1)
            nc.vector.tensor_copy(dst_idx[:, 1, :], dst_i[:, NG_COLS:2 * NG_COLS]).then_inc(dsti_ready, 1)

            dve.wait_ge(s_cnt, 1)
            link(nc.vector.tensor_copy(tot[:].rearrange("p b j -> p (b j)"), bank[0][:, 0:BK * NG_COLS]))
            link(nc.vector.tensor_reduce(cnt[:], tot[:], AX.X, ALU.add))
            link(nc.vector.tensor_scalar(cnt_i[:], cnt[:], float(SUPER - 1), None, ALU.add))
            link(nc.vector.tensor_scalar(cnt_i[:], cnt_i[:], 9, None, ALU.logical_shift_right))
            link(nc.vector.tensor_scalar(nsup[:], cnt_i[:], 1.0, None, ALU.max))
            link(nc.vector.tensor_tensor_scan(sup_end[:], nsup[:], nsup[:], 0.0, ALU.add, ALU.bypass))
            link(nc.vector.tensor_tensor(sup_start[:], sup_end[:], nsup[:], ALU.subtract))
            totf = tot[:].rearrange("p b j -> p (b j)")
            link(nc.vector.tensor_tensor_scan(cum[:], totf, totf, 0.0, ALU.add, ALU.bypass))
            link(nc.vector.tensor_tensor(excl[:].rearrange("p b j -> p (b j)"), cum[:], totf, ALU.subtract))
            link(nc.vector.scalar_tensor_tensor(shift[:], sup_start[:], float(SUPER), excl[:, :, 0], ALU.mult, ALU.subtract))
            nc.vector.tensor_tensor(base[:], excl[:], shift[:].unsqueeze(2).to_broadcast([P, BK, NG_COLS]), ALU.add).then_inc(s_base, 1)
            dve.wait_ge(s_col, 1)
            link(nc.vector.tensor_copy(start_col[:], bank[1][0:BK, 0:1]))
            nc.vector.tensor_scalar(reached[:], iota_sup[0:BK, :], start_col[:], None, ALU.is_ge).then_inc(s_reach, 1)
            nc.vector.tensor_scalar(last_f[:, 0:NB], sup_end[:, 0:NB], -1.0, float(P), ALU.add, ALU.mult)
            link(nc.vector.tensor_scalar(last_f[:, NB:2 * NB], iota_sup[:, 0:NB], sup_end[:, NB - 1:NB], float(P), ALU.add, ALU.mult))
            link(nc.vector.tensor_scalar(last_idx[:], last_f[:], iota_col[:], None, ALU.add))
            dve.wait_ge(s_blk, 1)
            link(nc.vector.tensor_scalar(blk[:], bank[2][:, 0:NS], -1.0, None, ALU.add))
            nc.vector.memset(same[:, 0:1], 0.0)
            nc.vector.tensor_tensor(same[:, 1:NS], blk[:, 1:NS], blk[:, 0:NS - 1], ALU.is_equal)
            link(nc.vector.tensor_scalar(blk_p[:], blk[:], float(P), None, ALU.mult))
            link(nc.vector.tensor_scalar(blk_idx[:], blk_p[:], iota_col[:], None, ALU.add))
            nc.vector.memset(ssq[:], 1.0).then_inc(s_tabs, 1)

            def dst_step(g, k, u):
                if not (isinstance(g, int) and g < RING):
                    dve.wait_ge(b_ready[k], u * 16 * NG_COLS)
                nc.vector.tensor_copy(dst_idx[:, k, :], dst_i[:, bass.ds(g * NG_COLS, NG_COLS)]).then_inc(dsti_ready, 1)

            def step(g, k, u, first):
                dve.wait_ge(rank_mm, g + 1)
                if not (isinstance(g, int) and g == 0):
                    dve.wait_ge(pos_ready, g)
                nc.vector.tensor_tensor(prod[:], bank[1][:, 0:BK * NG_COLS].rearrange("p (b j) -> p b j", j=NG_COLS),
                                            onehot[:, :, bass.ds(g * NG_COLS, NG_COLS)], ALU.mult).then_inc(rank_read, 1)
                dve.wait_ge(rank_read, g + 1)
                if not first:
                    dve.wait_ge(st_free[k], u * 16 * NG_COLS)
                with nc.allow_low_precision(reason="integers below 2**24"):
                    nc.vector.tensor_reduce(pos_idx[:, k, :], prod[:].rearrange("p b j -> p j b"), AX.X, ALU.add).then_inc(pos_ready, 1)
                if not (isinstance(g, int) and g + 2 >= NG):
                    dst_step(g + 2, (k + 2) % RING, u + (k + 2) // RING)
                dve.wait_ge(b_ready[k], (u + 1) * 16 * NG_COLS)
                for h in range(2):
                    dve.wait_ge(h_done, 2 * g + h + 1)
                    nc.vector.tensor_tensor(stage[:, k, 4 * h:4 * h + 4, 0:D],
                                            bank[6 + h][:].rearrange("p (t d) -> p t d", t=4),
                                            b_rows[:, k, 4 * h:4 * h + 4, :], ALU.add).then_inc(st_ready, 1)
            group_trips(dve, step)

            def step(n, k, i):
                if inside(n, 3):
                    s, kk = n + 3, (k + 3) % RING
                    if not early(n, 3, RING):
                        dve.wait_ge(a_ready[kk], (i + (k + 3) // RING) * 16)
                    nc.vector.tensor_copy(blk_now[:, kk:kk + 1], blk_idx[:, bass.ds(s, 1)]).then_inc(n_idx, 1)
                if inside(n, 1):
                    s, b2, kk = n + 1, (k + 1) % 2, (k + 1) % RING
                    dve.wait_ge(hs_ready[kk], (i + (k + 1) // RING) * 16 + 16)
                    if not early(n, 1, RING):
                        dve.wait_ge(n_o, s - RING + 1)
                    for j in range(SJ):
                        a = nc.vector.tensor_scalar(sel[kk][:, j, :], iota_row[:], hs[kk][:, j, D:ROW], None, ALU.is_equal)
                    a.then_inc(n_sel, 1)
                if inside(n, 0):
                    s, b2 = n, k % 2
                    dve.wait_ge(n_a, s + 1)
                    if not early(n, 0, 2):
                        dve.wait_ge(n_ssq, s - 1)
                        dve.wait_ge(n_dve, s - 1)
                    nc.vector.tensor_tensor(pre[b2], bank[2 + b2][:].rearrange("p (j d) -> p j d", j=SJ),
                                            hs[k][:, :, 0:D], ALU.add).then_inc(n_pre, 1)
                if inside(n, -1):
                    s, b2 = n - 1, (k + 1) % 2
                    dve.wait_ge(n_std, s + 1)
                    nc.vector.reciprocal(rstd[:, b2, :], std[:, b2, :]).then_inc(n_rs, 1)
                    dve.wait_ge(n_rs, s + 1)
                    if not early(n, -1, 2):
                        dve.wait_ge(n_o, s - 1)
                    for j in range(SJ):
                        a = nc.vector.scalar_tensor_tensor(msg[b2][:, j, :], pre[b2][:, j, :], rstd[:, b2, j:j + 1],
                                                           gamma_s[:], ALU.mult, ALU.mult)
                    a.then_inc(n_dve, 1)
                    dve.wait_ge(n_dve, s + 1)
                    nc.vector.tensor_tensor(msg[b2], msg[b2], beta_bc.unsqueeze(1).to_broadcast([P, SJ, D]),
                                            ALU.add).then_inc(n_norm, 1)
                if inside(n, -2):
                    s, kk = n - 2, (k - 2) % RING
                    dve.wait_ge(n_o, s + 1)
                    if not early(n, -2, 1):
                        dve.wait_ge(n_run, s)
                    if not early(n, -2, RING):
                        dve.wait_ge(run_st[kk], (i + (k - 2) // RING) * 16)
                    nc.vector.scalar_tensor_tensor(run[:, kk, :], run[:, (kk - 1) % RING, :], same[:, bass.ds(s, 1)],
                                                   bank[4 + kk % 2][:, 0:D], ALU.mult, ALU.add).then_inc(n_run, 1)
            super_trips(dve, step)

            nc.vector.memset(xr[:, NB - 1, :], 0.0).then_inc(f_ss, 1)
            for c in range(NCH):
                lo, hi = c * CH, (c + 1) * CH
                yc = y[:, lo:hi, :]
                dve.wait_ge(f_x[c], 16 if c < NCH - 1 else 32)
                dve.wait_ge(f_g[c], 16 * CH)
                nc.vector.tensor_tensor(yc, yc, xr[:, lo:hi, :], ALU.add).then_inc(f_dve, 1)
                dve.wait_ge(f_dve, 3 * c + 1)
                link(nc.vector.tensor_reduce(ysum[:, lo:hi], yc, AX.X, ALU.add))
                nc.vector.tensor_scalar(ymean[:, lo:hi], ysum[:, lo:hi], 1.0 / D, None, ALU.mult).then_inc(f_dve, 1)
                dve.wait_ge(f_dve, 3 * c + 2)
                nc.vector.tensor_tensor(yc, yc, ymean[:, lo:hi].unsqueeze(2).to_broadcast([P, CH, D]), ALU.subtract).then_inc(f_dve, 1)
                dve.wait_ge(f_sq, c + 1)
                nc.vector.tensor_reduce(yssq[:, lo:hi], y2[:, lo:hi, :], AX.X, ALU.add).then_inc(f_ss, 1)
                dve.wait_ge(f_sd, c + 1)
                link(nc.vector.reciprocal(yrstd[:, lo:hi], ystd[:, lo:hi]))
                link(nc.vector.tensor_scalar(yrstd[:, lo:hi], yrstd[:, lo:hi], float(D) ** 0.5, None, ALU.mult))
                nc.vector.tensor_tensor(yc, yc, yrstd[:, lo:hi].unsqueeze(2).to_broadcast([P, CH, D]), ALU.mult).then_inc(f_y, 1)


_INS = ['x', 'src', 'dst', 'edge_attr_128', 'L0_gnn_W', 'L0_gnn_b', 'L0_gnn_gamma', 'L0_gnn_beta']
_OUTS = [((6250, 128), 'float32')]


def kernel(**inputs):
    import numpy as _np
    import concourse.bacc as _bacc
    from concourse import mybir as _mybir
    from concourse.bass_utils import run_bass_kernel_spmd as _run

    nc = _bacc.Bacc("TRN2", target_bir_lowering=False, num_devices=1)
    arrays, args = {}, []
    for name in _INS:
        a = _np.ascontiguousarray(inputs[name])
        arrays[f"in_{name}_dram"] = a
        args.append(nc.dram_tensor(f"in_{name}_dram", a.shape, _mybir.dt.from_np(a.dtype), kind="ExternalInput").ap())
    for i, (shape, dtype) in enumerate(_OUTS):
        dt = _mybir.dt.from_np(_np.dtype(dtype))
        args.append(nc.dram_tensor(f"out_{i}_dram", shape, dt, kind="ExternalOutput").ap())
    bass_gnn_resnorm(nc, *args)
    r = _run(nc, [arrays], core_ids=[0])
    got = tuple(r.results[0][f"out_{i}_dram"] for i in range(len(_OUTS)))
    return got[0]
```

```python
import concourse.bass as bass
from concourse import mybir
from contextlib import ExitStack

F32 = mybir.dt.float32
BF16 = mybir.dt.bfloat16
I32 = mybir.dt.int32
ALU = mybir.AluOpType
ACT = mybir.ActivationFunctionType
AX = mybir.AxisListType

P = 128
D = 128
LN_EPS = 1e-5
NG_COLS = 8
GE = P * NG_COLS
SUPER = 512
SJ = SUPER // P
ROW = D + 1
RING = 4


def bass_gnn_resnorm(nc, x, src, dst, edge, W, b, gamma, beta, out):
    N = x.shape[0]
    E = src.shape[0]
    NB = -(-N // P)
    N_LAST = N - (NB - 1) * P
    NG = -(-E // GE)
    OVER = NG * GE - E
    C = NG * NG_COLS
    BK = NB + 1
    NS = (E + NB * SUPER) // SUPER
    NS_ALL = NS + RING
    assert OVER % NG_COLS == 0 and NG % 2 == 0 and E % GE != 0

    MIN_TRIPS = NB // RING
    W_MAX = NB * P - P

    tabA = nc.dram_tensor("tabA", (NB * P, D), F32)
    tabB = nc.dram_tensor("tabB", (NB * P, D), F32)
    rows = nc.dram_tensor("rows", ((NS_ALL + 1) * SUPER, ROW), F32)
    rows_ap = rows.ap()
    rows_quads = rows_ap.rearrange("(r j) c -> r (j c)", j=SJ)
    rows_super = rows_ap.rearrange("(s p j) c -> s p (j c)", p=P, j=SJ)
    tabA_v = tabA.ap().rearrange("(t p) d -> p t d", p=P)
    tabB_v = tabB.ap().rearrange("(t p) d -> p t d", p=P)
    x_v = x[0:(NB - 1) * P, :].rearrange("(t p) d -> p t d", p=P)
    out_v = out[0:(NB - 1) * P, :].rearrange("(t p) d -> p t d", p=P)
    edge_groups = edge[0:(NG - 1) * GE, :].rearrange("(g p j) d -> g p (j d)", p=P, j=NG_COLS)
    edge_last = edge[E - GE:E, :].rearrange("(p j) d -> p (j d)", j=NG_COLS)

    ctx = ExitStack()
    with ctx:
        def sb(name, shape, dt=F32):
            return ctx.enter_context(nc.sbuf_tensor(name, shape, dt))

        def sem(name):
            return ctx.enter_context(nc.semaphore(name))

        def sems(name, n):
            return [sem(f"{name}{i}") for i in range(n)]

        bank = [ctx.enter_context(nc.psum_tensor(f"bank{i}", [P, 512], F32)) for i in range(8)]

        iota_row = sb("iota_row", [P, P])
        iota_col = sb("iota_col", [P, 1])
        iota_sup = sb("iota_sup", [P, NS_ALL])
        ident = sb("ident", [P, P])
        before = sb("before", [P, P], BF16)
        not_before = sb("not_before", [P, P], BF16)
        ones_bf = sb("ones_bf", [P, P], BF16)
        ones_row = sb("ones_row", [1, P])
        eps128 = sb("eps128", [P, 1])
        w_sb = sb("w_sb", [P, 3, D])
        w_mean = sb("w_mean", [P, 3])
        wc = sb("wc", [P, 3, D])
        vecs = sb("vecs", [P, 3, D])
        b_mean = sb("b_mean", [P, 1])
        bc = sb("bc", [P, D])
        neg_beta = sb("neg_beta", [P, D])
        gamma_s = sb("gamma_s", [P, D])
        gb = vecs[:, 1, :]
        beta_bc = vecs[:, 2, :]
        w_low = sb("w_low", [NG, 1])
        w_high = sb("w_high", [NG, 1])
        w_diag = sb("w_diag", [NG, NG + 1])
        w_bc = sb("w_bc", [P, NG + 1])
        w_i = sb("w_i", [1, NG + 1], I32)
        dst_rel = sb("dst_rel", [P, C])
        src_i = sb("src_i", [P, C], I32)
        dst_i = sb("dst_i", [P, C], I32)
        lo_i = sb("lo_i", [P, C], I32)
        hi_bf = sb("hi_bf", [P, C], BF16)
        lo_f = sb("lo_f", [P, C])
        onehot = sb("onehot", [P, BK, C], BF16)
        tot = sb("tot", [P, BK, NG_COLS])
        cum = sb("cum", [P, BK * NG_COLS])
        excl = sb("excl", [P, BK, NG_COLS])
        cnt = sb("cnt", [P, BK])
        cnt_i = sb("cnt_i", [P, BK], I32)
        nsup = sb("nsup", [P, BK])
        sup_end = sb("sup_end", [P, BK])
        sup_start = sb("sup_start", [P, BK])
        shift = sb("shift", [P, BK])
        base = sb("base", [P, BK, NG_COLS])
        start_col = sb("start_col", [BK, 1])
        reached = sb("reached", [BK, NS_ALL])
        ones_f = sb("ones_f", [P, P])
        trips_i = sb("trips_i", [1, 1], I32)
        blk = sb("blk", [P, NS_ALL])
        last_f = sb("last_f", [P, NB + RING])
        last_idx = sb("last_idx", [P, NB + RING], I32)
        blk_i = sb("blk_i", [1, NS_ALL], I32)
        trips = sb("trips", [1, 1], I32)
        fill = sb("fill", [P, SJ, ROW])
        xq = sb("xq", [P, 2, 4, D])
        x_last = sb("x_last", [P, D])
        xT = sb("xT", [P, 2, 512])
        ab_st = sb("ab_st", [P, 2, 4, 2, D])
        e_sb = sb("e_sb", [P, RING, GE])
        eT = sb("eT", [P, 2, 512])
        b_rows = sb("b_rows", [P, RING, NG_COLS, D])
        b_win = [b_rows[:, k, 0, :] for k in range(RING)]
        hot_d = b_rows[:, 0:2, 1:5, :]
        hot_dT = [b_rows[:, 2 + h, 1:5, :].rearrange("p t d -> p (t d)") for h in range(2)]
        stage_room = sb("stage_room", [P, RING * NG_COLS * ROW])
        stage = stage_room[:].rearrange("p (k j c) -> p k j c", k=RING, j=NG_COLS)
        prod = sb("prod", [P, BK, NG_COLS])
        pos_idx = sb("pos_idx", [P, RING, NG_COLS], I32)
        idx_rows = b_rows[0:NG, 0:2, :, :].rearrange("p v t d -> p v (t d)").bitcast(I32)
        idx_f = stage_room[0:NG, 0:2 * GE].rearrange("p (v e) -> p v e", v=2)
        hi_i = dst_i
        dst_idx = sb("dst_idx", [P, RING, NG_COLS], I32)
        hs = [stage[:, k, 0:SJ, :] for k in range(RING)]
        quads = [e_sb[:, k // 2, 512 * (k % 2):512 * (k % 2) + 512] for k in range(2 * RING)]
        sel = [q.rearrange("p (j n) -> p j n", j=SJ) for q in quads[0:4]]
        selT = quads[4:6]
        pre = [q.rearrange("p (j n) -> p j n", j=SJ) for q in quads[6:8]]
        msg_room = b_rows[:].rearrange("p k j d -> p k (j d)")[:, :, 0:SJ * ROW].rearrange("p k (j c) -> p k j c", j=SJ)
        msg = [msg_room[:, k, :, :] for k in range(RING)]
        DVE_J = 3
        ssq = sb("ssq", [P, 2, SJ])
        std = sb("std", [P, 2, SJ])
        rstd = sb("rstd", [P, 2, SJ])
        CH = 7
        NCH = NB // CH
        assert NCH * CH == NB
        room = onehot[:].rearrange("p b c -> p (b c)").bitcast(F32)
        sums = room[:, 0:NB * ROW].rearrange("p (t c) -> p t c", t=NB)
        y = sums[:, :, 0:D]
        tabA_sb, y2 = (room[:, NB * (ROW + i * D):NB * (ROW + i * D + D)].rearrange("p (t d) -> p t d", t=NB) for i in range(2))
        ysum = sb("ysum", [P, NB])
        ymean = sb("ymean", [P, NB])
        yssq = sb("yssq", [P, NB])
        ystd = sb("ystd", [P, NB])
        yrstd = sb("yrstd", [P, NB])

        s_iota = sem("iota_made")
        s_const = sem("constants_made")
        s_win = sem("windows_found")
        s_wbc = sem("windows_broadcast")
        w_ready = sems("b_window_loaded", RING)
        hd_made = sem("dst_selectors_made")
        hd_t = sem("dst_selectors_transposed")
        hd_c = sem("dst_selectors_copied")
        n_scaled = sem("gamma_multiplied")
        n_cnt = sem("count_columns_cleared")
        n_selp = sem("pool_selectors_made")
        s_idx_in = sem("src_loaded")
        s_dst_in = sem("dst_loaded")
        s_last = sem("last_supertiles_known")
        s_idx_f = sem("indices_as_float")
        s_idx_t = sem("indices_transposed")
        s_dve = sem("dve_chain")
        s_hot = sem("onehot_made")
        s_cnt = sem("counts_summed")
        s_base = sem("bases_made")
        s_col = sem("starts_transposed")
        s_reach = sem("starts_compared")
        s_blk = sem("blocks_summed")
        s_tabs = sem("index_tables_made")
        s_fillv = sem("fill_rows_made")
        s_fill = sem("fills_landed")
        s_w = sem("weights_loaded")
        s_wc = sem("weights_centred")
        s_xz = sem("last_block_cleared")
        s_x = sems("x_quad_loaded", 2)
        s_xl = sem("last_block_loaded")
        s_xt = sem("x_transposed")
        s_xc = sem("xT_copied")
        s_ab = sem("tables_multiplied")
        s_ac = sem("tables_copied")
        s_bb = sem("bias_added")
        s_tab = sems("tables_stored", 2)
        s_turn = sem("pool_turns")
        e_ready = sems("e_loaded", RING)
        e_used = sem("e_transposed")
        eT_ready = sem("eT_copied")
        h_done = sem("edges_multiplied")
        rank_mm = sem("ranks_summed")
        rank_read = sem("ranks_read")
        pos_ready = sem("positions_made")
        dsti_ready = sem("dst_indices_made")
        b_ready = sems("b_rows_gathered", RING)
        lo_ready = sem("node_numbers_staged")
        st_ready = sem("rows_staged")
        st_free = sems("rows_scattered", RING)
        hs_ready = sems("hs_loaded", RING)
        a_ready = sems("a_table_loaded", 2)
        y_ready = sem("x_in_place")
        n_sel = sem("selectors_made")
        n_selT = sem("selectors_transposed")
        n_selTc = sem("selT_copied")
        n_a = sem("a_rows_selected")
        n_pre = sem("pre_made")
        n_ssq = sem("squares_summed")
        n_std = sem("std_made")
        n_msg = sem("messages_made")
        n_o = sem("messages_summed")
        n_run = sem("runs_made")
        n_rs = sem("rstd_made")
        tr_half = sem("e_first_half_transposed")
        f_dve = sem("final_chain")
        f_sq = sem("final_squared")
        f_ss = sem("final_sums")
        f_sd = sem("final_std")
        f_y = sem("final_rows")
        f_out = sem("output_stored")

        NQ = (NB - 1) // 4
        NIT = NG // RING
        LAST = NG - NIT * RING
        CNT = 7
        assert NQ * 4 == NB - 1 and NQ % 2 == 0 and NG % CNT == 0

        def zeroth(g):
            return isinstance(g, int) and g == 0

        def below(n, d, lim):
            return isinstance(n, int) and n + d < lim

        def group_trips(eng, step):
            for k in range(RING):
                step(k, k, 0)
            with eng.Fori(1, NIT) as i:
                for k in range(RING):
                    step(i * RING + k, k, i)
            for k in range(LAST):
                step(NIT * RING + k, k, NIT)

        def super_trips(eng, n_trips, step):
            for n in range(-3, RING):
                step(n, n % RING, n // RING, lambda lag, n=n: n + lag >= 0)
            with eng.Fori(1, n_trips - 1) as i:
                for k in range(RING):
                    step(i * RING + k, k, i, lambda lag: True)
            for t in range(-RING, 3):
                k = t % RING
                step(n_trips * RING + t, k, n_trips + t // RING, lambda lag, t=t: t + lag < 0)

        def few_windows(eng):
            wide = eng.alloc_register("wide_groups")
            eng.reg_load(wide, w_i[0:1, NG:NG + 1])
            return wide

        def trip_count(eng):
            return eng.value_load(trips[0:1, 0:1], min_val=0, max_val=NS_ALL // RING - MIN_TRIPS) + MIN_TRIPS

        block = ctx.enter_context(nc.Block())

        @block.sync
        def _(sp):
            sp.dma_start(idx_rows[0:NG - 2, 0, :], src[0:(NG - 2) * GE].rearrange("(g e) -> g e", e=GE)).then_inc(s_idx_in, 16)
            sp.dma_start(idx_rows[NG - 2:NG - 1, 0, :], src[(NG - 2) * GE:(NG - 1) * GE].rearrange("(g e) -> g e", g=1)).then_inc(s_idx_in, 16)
            sp.dma_start(idx_rows[NG - 1:NG, 0, :], src[E - GE:E].rearrange("(g e) -> g e", g=1)).then_inc(s_idx_in, 16)
            sp.dma_start(w_sb[:], W.rearrange("(t p) d -> p t d", p=P)).then_inc(s_w, 16)

            def quad(q, k, first):
                if not first:
                    sp.wait_ge(s_xt, q - 1)
                sp.dma_start(xq[:, k, :, :], x_v[:, bass.ds(q * 4, 4), :]).then_inc(s_x[k], 16)

            def store(q, k):
                sp.wait_ge(s_ac, 2 * q + 2)
                sp.dma_start(tabA_v[:, bass.ds(q * 4, 4), :], ab_st[:, k, :, 0, :]).then_inc(s_tab[k], 16)
                sp.wait_ge(s_bb, q + 1)
                sp.dma_start(tabB_v[:, bass.ds(q * 4, 4), :], ab_st[:, k, :, 1, :]).then_inc(s_tab[k], 16)

            quad(0, 0, True)
            quad(1, 1, True)
            sp.wait_ge(s_xz, 1)
            sp.dma_start(x_last[0:N_LAST, :], x[(NB - 1) * P:N, :]).then_inc(s_xl, 16)

            def load_edges(g, k):
                if not below(g, 0, RING):
                    sp.wait_ge(e_used, g - RING + 1)
                last = isinstance(g, int) and g == NG - 1
                sp.dma_start(e_sb[:, k, :], edge_last if last else edge_groups[g]).then_inc(e_ready[k], 16)

            for k in range(RING):
                load_edges(k, k)
            for k in range(2):
                store(k, k)
                quad(k + 2, k, False)
            with sp.Fori(1, NQ // 2 - 1) as i:
                for k in range(2):
                    store(2 * i + k, k)
                    quad(2 * i + 2 + k, k, False)
            for k in range(2):
                store(NQ - 2 + k, k)
            sp.wait_ge(s_ac, 2 * NQ + 1)
            sp.dma_start(tabA_v[:, NB - 1, :], ab_st[:, 0, 0, 0, :]).then_inc(s_tab[0], 16)
            sp.wait_ge(s_bb, NQ + 1)
            sp.dma_start(tabB_v[:, NB - 1, :], ab_st[:, 0, 0, 1, :]).then_inc(s_tab[0], 16)
            sp.wait_ge(s_tab[0], 16 * (NQ + 2))
            sp.wait_ge(s_tab[1], 16 * NQ)
            sp.wait_ge(s_tabs, 1)

            with sp.If_eq(few_windows(sp), 0):
                def load_window(g, k):
                    if not below(g, 0, RING):
                        sp.wait_ge(h_done, 2 * (g - RING) + 2)
                    at = sp.value_load(w_i[0:1, bass.ds(g, 1)], min_val=0, max_val=W_MAX)
                    sp.dma_start(b_win[k], tabB.ap()[bass.ds(at, P), :]).then_inc(w_ready[k], 16)

                def step(g, k, u):
                    if not below(g, 0, RING):
                        load_edges(g, k)
                    load_window(g, k)
                group_trips(sp, step)
            with sp.Else():
                def step(g, k, u):
                    if not below(g, 0, RING):
                        load_edges(g, k)
                group_trips(sp, step)

            n_trips = trip_count(sp)
            for k in range(RING):
                sp.wait_ge(st_free[k], 16 * NG_COLS * (NIT + (k < LAST)))

            HEAD = RING + 1
            sp.dma_start(tabA_sb[:, 0:HEAD, :], tabA_v[:, 0:HEAD, :]).then_inc(a_ready[0], 16)

            def step(n, k, i, on):
                if on(3):
                    s, kk = n + 3, (k + 3) % RING
                    if not below(n, 3, RING):
                        sp.wait_ge(n_pre, s - RING + 1)
                    sp.dma_start(hs[kk], rows_super[s]).then_inc(hs_ready[kk], 16)
                if isinstance(n, int) and n == 0:
                    sp.dma_start(y[:, 0:NB - 1, :], x_v).then_inc(y_ready, 16)
                    sp.dma_start(tabA_sb[:, HEAD:NB, :], tabA_v[:, HEAD:NB, :]).then_inc(a_ready[1], 16)
            super_trips(sp, n_trips, step)

            for c in range(NCH):
                lo, hi = c * CH, (c + 1) * CH
                sp.wait_ge(f_y, c + 1)
                if c < NCH - 1:
                    sp.dma_start(out_v[:, lo:hi, :], y[:, lo:hi, :]).then_inc(f_out, 16)
                else:
                    sp.dma_start(out_v[:, lo:hi - 1, :], y[:, lo:hi - 1, :]).then_inc(f_out, 16)
                    sp.dma_start(out[(NB - 1) * P:N, :], y[0:N_LAST, hi - 1, :]).then_inc(f_out, 16)
            sp.wait_ge(f_out, 16 * (NCH + 1))

        @block.gpsimd
        def _(pool):
            nc.gpsimd.iota(iota_row[:], [[1, P]], base=0, channel_multiplier=0,
                           allow_small_or_imprecise_dtypes=True).then_inc(s_iota, 1)
            nc.gpsimd.iota(iota_col[:], [[0, 1]], base=0, channel_multiplier=1,
                           allow_small_or_imprecise_dtypes=True).then_inc(s_iota, 1)
            nc.gpsimd.iota(iota_sup[:], [[1, NS_ALL]], base=0, channel_multiplier=0,
                           allow_small_or_imprecise_dtypes=True).then_inc(s_iota, 1)
            nc.gpsimd.memset(x_last[:], 0.0).then_inc(s_xz, 1)
            nc.gpsimd.memset(ones_bf[:], 1.0).then_inc(s_const, 1)
            nc.gpsimd.memset(ones_row[:], 1.0).then_inc(s_const, 1)
            nc.gpsimd.memset(ones_f[:], 1.0).then_inc(s_const, 1)
            nc.gpsimd.memset(eps128[:], D * LN_EPS).then_inc(s_const, 1)
            nc.gpsimd.memset(fill[:], 0.0).then_inc(s_fillv, 1)
            pool.wait_ge(s_fillv, 1)
            nc.gpsimd.memset(fill[:, :, D:ROW], -1.0).then_inc(s_fillv, 1)

            def settle():
                pool.sem_inc(s_turn, 1)

            pool.wait_ge(s_last, 1)
            pool.wait_ge(s_fillv, 2)
            fill_rows = fill[:].rearrange("p j c -> p (j c)")
            for t in range(NB + RING):
                nc.gpsimd.indirect_dma_start(rows_quads, bass.IndirectOffsetOnAxis(last_idx[:, t:t + 1], 0),
                                             fill_rows, None).then_inc(s_fill, 16)

            pool.wait_ge(s_tabs, 1)
            pool.wait_ge(s_fill, 16 * (NB + RING))

            def scatter(g, k):
                pool.wait_ge(pos_ready, g + 1)
                pool.wait_ge(lo_ready, g + 1)
                pool.wait_ge(st_ready, 2 * g + 2)
                settle()
                for j in range(NG_COLS):
                    nc.gpsimd.indirect_dma_start(rows_ap, bass.IndirectOffsetOnAxis(pos_idx[:, k, j:j + 1], 0),
                                                 stage[:, k, j, :], None).then_inc(st_free[k], 16)

            with pool.If_eq(few_windows(pool), 0):
                group_trips(pool, lambda g, k, u: scatter(g, k))
            with pool.Else():
                pool.wait_ge(s_tab[0], 16 * (NQ + 2))
                pool.wait_ge(s_tab[1], 16 * NQ)

                def gather_b(g, k):
                    pool.wait_ge(dsti_ready, g + 1)
                    if not below(g, 0, RING):
                        pool.wait_ge(st_ready, 2 * (g - RING) + 2)
                    settle()
                    for j in range(NG_COLS):
                        nc.gpsimd.indirect_dma_start(b_rows[:, k, j, :], None, tabB.ap(),
                                                     bass.IndirectOffsetOnAxis(dst_idx[:, k, j:j + 1], 0)).then_inc(b_ready[k], 16)

                def step(g, k, u):
                    if not (isinstance(g, int) and g + 2 >= NG):
                        gather_b(g + 2, (k + 2) % RING)
                    scatter(g, k)
                gather_b(0, 0)
                gather_b(1, 1)
                group_trips(pool, step)

            n_trips = trip_count(pool)

            def step(n, k, i, on):
                if on(0):
                    s = n
                    pool.wait_ge(n_pre, s + 1)
                    if not below(n, 0, RING):
                        pool.wait_ge(n_o, s - RING + 1)
                    nc.gpsimd.tensor_tensor(msg[k][:, :, 0:D], pre[k % 2], gamma_s[:].unsqueeze(1).to_broadcast([P, SJ, D]),
                                            ALU.mult).then_inc(n_scaled, 1)
                if on(2):
                    s, kk = n + 2, (k + 2) % RING
                    pool.wait_ge(hs_ready[kk], (i + (k + 2) // RING) * 16 + 16)
                    if not below(n, 2, RING):
                        pool.wait_ge(n_o, s - RING + 1)
                    settle()
                    for j in range(DVE_J, SJ):
                        a = nc.gpsimd.tensor_scalar(sel[kk][:, j, :], iota_row[:], hs[kk][:, j, D:ROW], None, ALU.is_equal)
                    a.then_inc(n_selp, 1)
            super_trips(pool, n_trips, step)

        @block.tensor
        def _(pe):
            pe.wait_ge(s_const, 5)
            for v in range(2):
                pe.wait_ge(s_idx_f, v + 1)
                for j in range(NG_COLS):
                    o = bank[2 * v + j // 4][:, 0:4 * NG].rearrange("p (j g) -> p j g", j=4)
                    mm = pe.transpose(o[:, j % 4, :], idx_f[:, v, j::NG_COLS], ident[0:NG, 0:NG])
                mm.then_inc(s_idx_t, 1)

            pe.wait_ge(s_hot, 1)

            def hot(g):
                return onehot[:, :, bass.ds(g * NG_COLS, NG_COLS)]

            total = bank[0][:, 0:BK * NG_COLS].rearrange("p (b j) -> p b j", j=NG_COLS)
            for g in range(CNT):
                pe.matmul(total, ones_bf[:], hot(g), start=(g == 0), stop=False)
            with pe.Fori(1, NG // CNT - 1) as i:
                for g in range(CNT):
                    pe.matmul(total, ones_bf[:], hot(i * CNT + g), start=False, stop=False)
            for g in range(NG - CNT, NG):
                mm = pe.matmul(total, ones_bf[:], hot(g), start=False, stop=(g == NG - 1))
            mm.then_inc(s_cnt, 1)
            pe.wait_ge(s_win, 1)
            pe.matmul(bank[1][:, 0:NG + 1], ones_f[0:NG, :], w_diag[:], start=True, stop=True).then_inc(s_wbc, 1)

            pe.wait_ge(s_wc, 1)

            def x_turn(q, k, u=None):
                if u is None:
                    pe.wait_ge(s_xl, 16)
                else:
                    pe.wait_ge(s_x[k], 16 * (u + 1))
                if not below(q, 0, 2):
                    pe.wait_ge(s_xc, q - 1)
                for t in range(1 if u is None else 4):
                    mm = pe.transpose(bank[4 + k][:, t * P:(t + 1) * P], x_last[:] if u is None else xq[:, k, t, :], ident[:])
                mm.then_inc(s_xt, 1)

            def x_mult(q, k, nblk=4):
                pe.wait_ge(s_xc, q + 1)
                if not below(q, 0, 2):
                    pe.wait_ge(s_ac, 2 * q - 2)
                for t in range(nblk):
                    mm = pe.matmul(bank[(6, 2)[k] + t // 2][:, (t % 2) * 256:(t % 2) * 256 + 256],
                                   xT[:, k, t * P:(t + 1) * P], wc[:, 0:2, :].rearrange("p t d -> p (t d)"),
                                   start=True, stop=True)
                mm.then_inc(s_ab, 1)

            x_turn(0, 0, 0)
            x_turn(1, 1, 0)
            x_mult(0, 0)
            pe.wait_ge(s_base, 1)
            pe.transpose(bank[0][0:BK, 0:P], sup_start[:], ident[:]).then_inc(s_col, 1)
            x_mult(1, 1)
            pe.wait_ge(s_reach, 1)
            pe.matmul(bank[0][:, P:P + NS_ALL], ones_f[0:NB, :], reached[0:NB, :], start=True, stop=True).then_inc(s_blk, 1)
            x_turn(2, 0, 1)
            with pe.Fori(1, NQ // 2 - 1) as i:
                x_turn(2 * i + 1, 1, i)
                x_mult(2 * i, 0)
                x_turn(2 * i + 2, 0, i + 1)
                x_mult(2 * i + 1, 1)
            x_turn(NQ - 1, 1, NQ // 2 - 1)
            x_mult(NQ - 2, 0)
            x_turn(NQ, 0)
            x_mult(NQ - 1, 1)
            x_mult(NQ, 0, 1)

            acc = bank[1][:, 0:BK * NG_COLS].rearrange("p (b j) -> p b j", j=NG_COLS)
            pe.wait_ge(s_tabs, 1)
            pe.matmul(bank[1][:, 0:BK * NG_COLS], ones_row[:], base[0:1, :, :].rearrange("p b j -> p (b j)"),
                      start=True, stop=False, skip_group_check=True)
            pe.wait_ge(s_ac, 2 * NQ + 1)

            def ranks(g):
                if not zeroth(g):
                    pe.wait_ge(rank_read, g)
                    pe.matmul(acc, not_before[:], hot(g - 1), start=False, stop=False, skip_group_check=True)
                pe.matmul(acc, before[:], hot(g), start=False, stop=True, skip_group_check=True).then_inc(rank_mm, 1)

            def turn_edges(g, k, u):
                pe.wait_ge(e_ready[k], u * 16 + 16)
                for h in range(2):
                    if not zeroth(g):
                        pe.wait_ge(eT_ready, 2 * g + h - 1)
                    for t in range(4):
                        j = 4 * h + t
                        mm = pe.transpose(bank[4 + h][:, t * P:(t + 1) * P], e_sb[:, k, j * D:(j + 1) * D], ident[:])
                    mm.then_inc((tr_half, e_used)[h], 1)

            with pe.If_eq(few_windows(pe), 0):
                def step(g, k, u):
                    for h in range(2):
                        pe.wait_ge(hd_made, 2 * g + h + 1)
                        if not zeroth(g):
                            pe.wait_ge(hd_c, 2 * g + h - 1)
                        for t in range(4):
                            mm = pe.transpose(bank[2 + h][:, t * P:(t + 1) * P], hot_d[:, h, t, :], ident[:])
                        mm.then_inc(hd_t, 1)
                    turn_edges(g, k, u)
                    ranks(g)
                    pe.wait_ge(w_ready[k], u * 16 + 16)
                    for h in range(2):
                        pe.wait_ge(hd_c, 2 * g + h + 1)
                        pe.wait_ge(eT_ready, 2 * g + h + 1)
                        if not zeroth(g):
                            pe.wait_ge(st_ready, 2 * g + h - 1)
                        for t in range(4):
                            pe.matmul(bank[6 + h][:, t * D:(t + 1) * D], eT[:, h, t * P:(t + 1) * P], wc[:, 2, :],
                                      start=True, stop=False)
                            mm = pe.matmul(bank[6 + h][:, t * D:(t + 1) * D], hot_dT[h][:, t * P:(t + 1) * P], b_win[k],
                                           start=False, stop=True)
                        mm.then_inc(h_done, 1)
                group_trips(pe, step)
            with pe.Else():
                def step(g, k, u):
                    ranks(g)
                    turn_edges(g, k, u)
                    for h in range(2):
                        pe.wait_ge(eT_ready, 2 * g + h + 1)
                        if not zeroth(g):
                            pe.wait_ge(st_ready, 2 * g + h - 1)
                        for t in range(4):
                            mm = pe.matmul(bank[6 + h][:, t * D:(t + 1) * D], eT[:, h, t * P:(t + 1) * P], wc[:, 2, :],
                                           start=True, stop=True)
                        mm.then_inc(h_done, 1)
                group_trips(pe, step)

            def step(n, k, i, on):
                if on(1):
                    s, b2 = n + 1, (k + 1) % 2
                    at = pe.value_load(blk_i[0:1, bass.ds(s, 1)], min_val=0, max_val=NB - 1)
                    pe.wait_ge(n_sel, s + 1)
                    pe.wait_ge(n_selp, s + 1)
                    if not below(n, 1, 2):
                        pe.wait_ge(n_selTc, s - 1)
                    for j in range(SJ):
                        mm = pe.transpose(bank[b2][:, j * P:(j + 1) * P], sel[(k + 1) % RING][:, j, :], ident[:])
                    mm.then_inc(n_selT, 1)
                if on(-2):
                    s, b2 = n - 2, k % 2
                    pe.wait_ge(n_msg, s + 1)
                    if not below(n, -2, 2):
                        pe.wait_ge(n_run, s - 1)
                    for j in range(SJ):
                        mm = pe.matmul(bank[4 + b2][:, 0:ROW], sel[(k - 2) % RING][:, j, :], msg[(k - 2) % RING][:, j, :],
                                       start=(j == 0), stop=(j == SJ - 1))
                    mm.then_inc(n_o, 1)
                if on(1):
                    s, b2 = n + 1, (k + 1) % 2
                    if isinstance(n, int) and n == -1:
                        pe.wait_ge(a_ready[0], 16)
                    if not isinstance(n, int) and k == 0:
                        pe.wait_ge(a_ready[1], 16)
                    pe.wait_ge(n_selTc, s + 1)
                    if not below(n, 1, 2):
                        pe.wait_ge(n_pre, s - 1)
                    for j in range(SJ):
                        mm = pe.matmul(bank[2 + b2][:, j * D:(j + 1) * D], selT[b2][:, j * P:(j + 1) * P], tabA_sb[:, bass.ds(at, 1), :],
                                       start=True, stop=True)
                    mm.then_inc(n_a, 1)
            super_trips(pe, trip_count(pe), step)

        @block.scalar
        def _(act):
            act.dma_start(idx_rows[0:NG - 2, 1, :], dst[0:(NG - 2) * GE].rearrange("(g e) -> g e", e=GE)).then_inc(s_dst_in, 16)
            act.dma_start(idx_rows[NG - 2:NG - 1, 1, :], dst[(NG - 2) * GE:(NG - 1) * GE].rearrange("(g e) -> g e", g=1)).then_inc(s_dst_in, 16)
            act.dma_start(idx_rows[NG - 1:NG, 1, :], dst[E - GE:E].rearrange("(g e) -> g e", g=1)).then_inc(s_dst_in, 16)
            for n, v in enumerate((b, gamma, beta)):
                act.dma_start(vecs[:, n, :], v.partition_broadcast(P)).then_inc(s_w, 16)

            def x_copy(q, k, nblk=4):
                act.wait_ge(s_xt, q + 1)
                if not below(q, 0, 2):
                    act.wait_ge(s_ab, q - 1)
                nc.scalar.copy(xT[:, k, 0:nblk * P], bank[4 + k][:, 0:nblk * P]).then_inc(s_xc, 1)

            def ab_copy(q, k, u, nblk=4):
                act.wait_ge(s_ab, q + 1)
                if not below(q, 0, 2):
                    act.wait_ge(s_tab[k], u * 32)
                for h in range(-(-nblk // 2)):
                    m = min(2, nblk)
                    o = bank[(6, 2)[k] + h][:, 0:m * 256].rearrange("p (t w d) -> p t w d", t=m, w=2)
                    nc.scalar.copy(ab_st[:, k, 2 * h:2 * h + m, :, :], o).then_inc(s_ac, 1)

            x_copy(0, 0)
            x_copy(1, 1)
            ab_copy(0, 0, 0)
            x_copy(2, 0)
            ab_copy(1, 1, 0)
            with act.Fori(1, NQ // 2 - 1) as i:
                x_copy(2 * i + 1, 1)
                ab_copy(2 * i, 0, i)
                x_copy(2 * i + 2, 0)
                ab_copy(2 * i + 1, 1, i)
            x_copy(NQ - 1, 1)
            ab_copy(NQ - 2, 0, NQ // 2 - 1)
            x_copy(NQ, 0, 1)
            ab_copy(NQ - 1, 1, NQ // 2 - 1)
            ab_copy(NQ, 0, NQ // 2, 1)

            act.wait_ge(s_tabs, 1)

            def number_rows(g, k, u):
                if not below(g, 0, RING):
                    act.wait_ge(st_free[k], u * 16 * NG_COLS)
                nc.scalar.copy(stage[:, k, :, D], lo_f[:, bass.ds(g * NG_COLS, NG_COLS)]).then_inc(lo_ready, 1)

            def copy_edges(g, k, u):
                for h in range(2):
                    act.wait_ge((tr_half, e_used)[h], g + 1)
                    if not zeroth(g):
                        act.wait_ge(h_done, 2 * g + h - 1)
                    nc.scalar.copy(eT[:, h, :], bank[4 + h][:]).then_inc(eT_ready, 1)

            with act.If_eq(few_windows(act), 0):
                def step(g, k, u):
                    for h in range(2):
                        act.wait_ge(hd_t, 2 * g + h + 1)
                        if not zeroth(g):
                            act.wait_ge(h_done, 2 * g + h - 1)
                        nc.scalar.copy(hot_dT[h], bank[2 + h][:]).then_inc(hd_c, 1)
                    copy_edges(g, k, u)
                    number_rows(g, k, u)
                    for h in range(2):
                        act.wait_ge(h_done, 2 * g + h + 1)
                        nc.scalar.copy(stage[:, k, 4 * h:4 * h + 4, 0:D],
                                       bank[6 + h][:].rearrange("p (t d) -> p t d", t=4)).then_inc(st_ready, 1)
                group_trips(act, step)
            with act.Else():
                def step(g, k, u):
                    copy_edges(g, k, u)
                    number_rows(g, k, u)
                group_trips(act, step)

            def step(n, k, i, on):
                if on(1):
                    s, b2 = n + 1, (k + 1) % 2
                    act.wait_ge(n_selT, s + 1)
                    if not below(n, 1, 2):
                        act.wait_ge(n_a, s - 1)
                    nc.scalar.copy(selT[b2], bank[b2][:]).then_inc(n_selTc, 1)
                if on(0):
                    s, b2 = n, k % 2
                    act.wait_ge(n_pre, s + 1)
                    if not below(n, 0, 2):
                        act.wait_ge(n_std, s - 1)
                    for j in range(SJ):
                        a = nc.scalar.activation(eT[:, b2, j * D:(j + 1) * D], pre[b2][:, j, :], ACT.Square,
                                                 accum_out=ssq[:, b2, j:j + 1])
                    a.then_inc(n_ssq, 1)
                    act.wait_ge(n_ssq, s + 1)
                    if not below(n, 0, 2):
                        act.wait_ge(n_rs, s - 1)
                    nc.scalar.activation(std[:, b2, :], ssq[:, b2, :], ACT.Sqrt, bias=eps128[:]).then_inc(n_std, 1)
            super_trips(act, trip_count(act), step)

            for c in range(NCH):
                lo, hi = c * CH, (c + 1) * CH
                act.wait_ge(f_dve, 3 * c + 3)
                nc.scalar.activation(y2[:, lo:hi, :], y[:, lo:hi, :], ACT.Square).then_inc(f_sq, 1)
                act.wait_ge(f_ss, c + 1)
                nc.scalar.activation(ystd[:, lo:hi], yssq[:, lo:hi], ACT.Sqrt, bias=eps128[:]).then_inc(f_sd, 1)

        @block.vector
        def _(dve):
            chain = [0]

            def link(ins):
                chain[0] += 1
                ins.then_inc(s_dve, 1)
                dve.wait_ge(s_dve, chain[0])

            dve.wait_ge(s_iota, 3)
            nc.vector.tensor_scalar(ident[:], iota_row[:], iota_col[:], None, ALU.is_equal).then_inc(s_const, 1)
            nc.vector.tensor_scalar(before[:], iota_row[:], iota_col[:], None, ALU.is_gt)
            nc.vector.tensor_scalar(not_before[:], iota_row[:], iota_col[:], None, ALU.is_le)
            dve.wait_ge(s_idx_in, 48)
            nc.vector.tensor_copy(idx_f[:, 0, :], idx_rows[:, 0, :]).then_inc(s_idx_f, 1)
            dve.wait_ge(s_dst_in, 48)
            nc.vector.tensor_copy(idx_f[:, 1, :], idx_rows[:, 1, :]).then_inc(s_idx_f, 1)
            dve.wait_ge(s_idx_t, 1)
            for h in range(2):
                o = src_i[:].rearrange("p (g j) -> p j g", j=NG_COLS)[:, 4 * h:4 * h + 4, :]
                a = nc.vector.tensor_copy(o, bank[h][:, 0:4 * NG].rearrange("p (j g) -> p j g", j=4))
            link(a)
            nc.vector.tensor_scalar(hi_i[:], src_i[:], 7, None, ALU.logical_shift_right)
            link(nc.vector.tensor_scalar(lo_i[:], src_i[:], P - 1, None, ALU.bitwise_and))
            link(nc.vector.tensor_copy(hi_bf[:], hi_i[:]))
            link(nc.vector.memset(hi_bf[0:OVER // NG_COLS, C - NG_COLS:C], float(NB)))
            for bk in range(BK):
                a = nc.vector.tensor_scalar(onehot[:, bk, :], hi_bf[:], float(bk), None, ALU.is_equal)
            a.then_inc(s_hot, 1)
            dve.wait_ge(s_w, 64)
            link(nc.vector.tensor_reduce(w_mean[:], w_sb[:], AX.X, ALU.add))
            link(nc.vector.tensor_scalar(w_mean[:], w_mean[:], 1.0 / D, None, ALU.mult))
            nc.vector.tensor_tensor(wc[:], w_sb[:], w_mean[:].unsqueeze(2).to_broadcast([P, 3, D]), ALU.subtract).then_inc(s_wc, 1)
            link(nc.vector.tensor_reduce(b_mean[:], vecs[:, 0, :], AX.X, ALU.add))
            link(nc.vector.tensor_scalar(b_mean[:], b_mean[:], 1.0 / D, None, ALU.mult))
            nc.vector.tensor_scalar(bc[:], vecs[:, 0, :], b_mean[:], None, ALU.subtract)
            nc.vector.tensor_scalar(neg_beta[:], beta_bc, -1.0, None, ALU.mult)
            nc.vector.tensor_scalar(gamma_s[:], gb, float(D) ** 0.5, None, ALU.mult)
            nc.vector.tensor_reduce(w_high[:], idx_f[:, 1, :], AX.X, ALU.max)
            link(nc.vector.tensor_reduce(w_low[:], idx_f[:, 1, :], AX.X, ALU.min))
            link(nc.vector.tensor_scalar(w_low[:], w_low[:], float(W_MAX), None, ALU.min))
            nc.vector.tensor_scalar(w_diag[:, 0:NG], ident[0:NG, 0:NG], w_low[:], None, ALU.mult)
            nc.vector.tensor_scalar(w_diag[:, NG:NG + 1], w_high[:], w_low[:], float(P - 1), ALU.subtract, ALU.is_gt).then_inc(s_win, 1)
            nc.vector.tensor_copy(lo_f[:], lo_i[:])
            dve.wait_ge(s_idx_t, 2)
            for h in range(2):
                o = dst_rel[:].rearrange("p (g j) -> p j g", j=NG_COLS)[:, 4 * h:4 * h + 4, :]
                a = nc.vector.tensor_copy(o, bank[2 + h][:, 0:4 * NG].rearrange("p (j g) -> p j g", j=4))
            link(a)
            link(nc.vector.tensor_copy(dst_i[:], dst_rel[:]))
            nc.vector.tensor_copy(dst_idx[:, 0, :], dst_i[:, 0:NG_COLS]).then_inc(dsti_ready, 1)
            nc.vector.tensor_copy(dst_idx[:, 1, :], dst_i[:, NG_COLS:2 * NG_COLS]).then_inc(dsti_ready, 1)
            dve.wait_ge(s_wbc, 1)
            nc.vector.tensor_copy(w_i[:], bank[1][0:1, 0:NG + 1])
            link(nc.vector.tensor_copy(w_bc[:], bank[1][:, 0:NG + 1]))
            dv = dst_rel[:].rearrange("p (g j) -> p g j", j=NG_COLS)
            nc.vector.tensor_tensor(dv, dv, w_bc[:, 0:NG].unsqueeze(2).to_broadcast([P, NG, NG_COLS]), ALU.subtract)

            dve.wait_ge(s_cnt, 1)
            link(nc.vector.tensor_copy(tot[:].rearrange("p b j -> p (b j)"), bank[0][:, 0:BK * NG_COLS]))
            link(nc.vector.tensor_reduce(cnt[:], tot[:], AX.X, ALU.add))
            link(nc.vector.tensor_scalar(cnt_i[:], cnt[:], float(SUPER - 1), None, ALU.add))
            link(nc.vector.tensor_scalar(cnt_i[:], cnt_i[:], 9, None, ALU.logical_shift_right))
            link(nc.vector.tensor_scalar(nsup[:], cnt_i[:], 1.0, None, ALU.max))
            link(nc.vector.tensor_tensor_scan(sup_end[:], nsup[:], nsup[:], 0.0, ALU.add, ALU.bypass))
            link(nc.vector.tensor_tensor(sup_start[:], sup_end[:], nsup[:], ALU.subtract))
            link(nc.vector.memset(sup_start[:, NB:BK], float(NS_ALL)))
            nc.vector.tensor_scalar(last_f[:, 0:NB], sup_end[:, 0:NB], -1.0, float(P), ALU.add, ALU.mult)
            link(nc.vector.tensor_scalar(last_f[:, NB:NB + RING], iota_sup[:, 0:RING], sup_end[:, NB - 1:NB], float(P), ALU.add, ALU.mult))
            nc.vector.tensor_scalar(last_idx[:], last_f[:], iota_col[:], None, ALU.add).then_inc(s_last, 1)
            totf = tot[:].rearrange("p b j -> p (b j)")
            link(nc.vector.tensor_tensor_scan(cum[:], totf, totf, 0.0, ALU.add, ALU.bypass))
            link(nc.vector.tensor_tensor(excl[:].rearrange("p b j -> p (b j)"), cum[:], totf, ALU.subtract))
            link(nc.vector.scalar_tensor_tensor(shift[:], sup_start[:], float(SUPER), excl[:, :, 0], ALU.mult, ALU.subtract))
            nc.vector.tensor_tensor(base[:], excl[:], shift[:].unsqueeze(2).to_broadcast([P, BK, NG_COLS]), ALU.add).then_inc(s_base, 1)
            link(nc.vector.tensor_scalar(trips_i[:], sup_end[0:1, NB - 1:NB], float(RING - 1), None, ALU.add))
            link(nc.vector.tensor_scalar(trips_i[:], trips_i[:], 2, None, ALU.logical_shift_right))
            nc.vector.tensor_scalar(trips[:], trips_i[:], float(-MIN_TRIPS), None, ALU.add)
            dve.wait_ge(s_col, 1)
            link(nc.vector.tensor_copy(start_col[:], bank[0][0:BK, 0:1]))
            nc.vector.tensor_scalar(reached[:], iota_sup[0:BK, :], start_col[:], None, ALU.is_ge).then_inc(s_reach, 1)
            dve.wait_ge(s_blk, 1)
            link(nc.vector.tensor_scalar(blk[:], bank[0][:, P:P + NS_ALL], -1.0, None, ALU.add))
            link(nc.vector.tensor_copy(blk_i[:], blk[0:1, :]))
            nc.vector.memset(ssq[:], 1.0).then_inc(s_tabs, 1)

            def bias(q, k, nblk=4):
                dve.wait_ge(s_ac, 2 * q + -(-nblk // 2))
                v = ab_st[:, k, 0:nblk, 1, :]
                nc.vector.tensor_tensor(v, v, bc[:].unsqueeze(1).to_broadcast([P, nblk, D]), ALU.add).then_inc(s_bb, 1)
            with dve.Fori(0, NQ // 2) as i:
                for k in range(2):
                    bias(2 * i + k, k)
            bias(NQ, 0, 1)

            def positions(g, k, u):
                dve.wait_ge(rank_mm, g + 1)
                if not zeroth(g):
                    dve.wait_ge(pos_ready, g)
                nc.vector.tensor_tensor(prod[:], bank[1][:, 0:BK * NG_COLS].rearrange("p (b j) -> p b j", j=NG_COLS),
                                        onehot[:, :, bass.ds(g * NG_COLS, NG_COLS)], ALU.mult).then_inc(rank_read, 1)
                dve.wait_ge(rank_read, g + 1)
                if not below(g, 0, RING):
                    dve.wait_ge(st_free[k], u * 16 * NG_COLS)
                with nc.allow_low_precision(reason="integers below 2**24"):
                    nc.vector.tensor_reduce(pos_idx[:, k, :], prod[:].rearrange("p b j -> p j b"), AX.X, ALU.add).then_inc(pos_ready, 1)

            with dve.If_eq(few_windows(dve), 0):
                def step(g, k, u):
                    for h in range(2):
                        if not zeroth(g):
                            dve.wait_ge(hd_t, 2 * g + h - 1)
                        nc.vector.tensor_tensor(hot_d[:, h, :, :], iota_row[:].unsqueeze(1).to_broadcast([P, 4, P]),
                                                dst_rel[:, bass.ds(g * NG_COLS + 4 * h, 4)].unsqueeze(2).to_broadcast([P, 4, P]),
                                                ALU.is_equal).then_inc(hd_made, 1)
                    positions(g, k, u)
                group_trips(dve, step)
            with dve.Else():
                def step(g, k, u):
                    positions(g, k, u)
                    if not (isinstance(g, int) and g + 2 >= NG):
                        kk = (k + 2) % RING
                        if not below(g, 2, RING):
                            dve.wait_ge(b_ready[kk], (u + (k + 2) // RING) * 16 * NG_COLS)
                        nc.vector.tensor_copy(dst_idx[:, kk, :], dst_i[:, bass.ds((g + 2) * NG_COLS, NG_COLS)]).then_inc(dsti_ready, 1)
                    dve.wait_ge(b_ready[k], (u + 1) * 16 * NG_COLS)
                    for h in range(2):
                        dve.wait_ge(h_done, 2 * g + h + 1)
                        nc.vector.tensor_tensor(stage[:, k, 4 * h:4 * h + 4, 0:D],
                                                bank[6 + h][:].rearrange("p (t d) -> p t d", t=4),
                                                b_rows[:, k, 4 * h:4 * h + 4, :], ALU.add).then_inc(st_ready, 1)
                group_trips(dve, step)

            def step(n, k, i, on):
                if on(0):
                    s, b2 = n, k % 2
                    dve.wait_ge(n_a, s + 1)
                    if not below(n, 0, 2):
                        dve.wait_ge(n_ssq, s - 1)
                        dve.wait_ge(n_scaled, s - 1)
                    nc.vector.tensor_tensor(pre[b2], bank[2 + b2][:].rearrange("p (j d) -> p j d", j=SJ),
                                            hs[k][:, :, 0:D], ALU.add).then_inc(n_pre, 1)
                if on(-1):
                    s, b2, kk = n - 1, (k + 1) % 2, (k - 1) % RING
                    dve.wait_ge(n_std, s + 1)
                    nc.vector.reciprocal(rstd[:, b2, :], std[:, b2, :]).then_inc(n_rs, 1)
                    dve.wait_ge(n_rs, s + 1)
                    dve.wait_ge(n_scaled, s + 1)
                    for j in range(SJ):
                        a = nc.vector.scalar_tensor_tensor(msg[kk][:, j, 0:D], msg[kk][:, j, 0:D], rstd[:, b2, j:j + 1],
                                                           neg_beta[:], ALU.mult, ALU.max)
                    a.then_inc(n_msg, 1)
                if on(-3):
                    s, b2 = n - 3, (k - 3) % 2
                    at = dve.value_load(blk_i[0:1, bass.ds(s, 1)], min_val=0, max_val=NB - 1)
                    dve.wait_ge(n_o, s + 1)
                    if below(n, -3, 1):
                        dve.wait_ge(y_ready, 16 + 1)
                    else:
                        dve.wait_ge(n_run, s)
                    yb = sums[:, bass.ds(at, 1), :].squeeze(1)
                    nc.vector.tensor_tensor(yb, yb, bank[4 + b2][:, 0:ROW], ALU.add).then_inc(n_run, 1)
                if on(2):
                    s, kk = n + 2, (k + 2) % RING
                    dve.wait_ge(hs_ready[kk], (i + (k + 2) // RING) * 16 + 16)
                    if not below(n, 2, RING):
                        dve.wait_ge(n_o, s - RING + 1)
                    nc.vector.tensor_tensor(sel[kk][:, 0:DVE_J, :], iota_row[:].unsqueeze(1).to_broadcast([P, DVE_J, P]),
                                            hs[kk][:, 0:DVE_J, D:ROW].to_broadcast([P, DVE_J, P]), ALU.is_equal).then_inc(n_sel, 1)
            for k in range(RING):
                dve.wait_ge(st_free[k], 16 * NG_COLS * (NIT + (k < LAST)))
            nc.vector.memset(msg_room[:, :, :, D:ROW], 1.0).then_inc(n_cnt, 1)
            nc.vector.memset(sums[:, :, D:ROW], 0.0).then_inc(n_cnt, 1)
            nc.vector.tensor_copy(y[:, NB - 1, :], x_last[:]).then_inc(y_ready, 1)
            dve.wait_ge(n_cnt, 2)
            n_trips = trip_count(dve)
            super_trips(dve, n_trips, step)

            dve.wait_ge(n_run, n_trips * RING)
            for c in range(NCH):
                lo, hi = c * CH, (c + 1) * CH
                yc, y2c = y[:, lo:hi, :], y2[:, lo:hi, :]
                nc.vector.tensor_tensor(y2c, sums[:, lo:hi, D:ROW].to_broadcast([P, CH, D]),
                                        beta_bc.unsqueeze(1).to_broadcast([P, CH, D]), ALU.mult).then_inc(f_dve, 1)
                dve.wait_ge(f_dve, 3 * c + 1)
                link(nc.vector.tensor_tensor(yc, yc, y2c, ALU.add))
                link(nc.vector.tensor_reduce(ysum[:, lo:hi], yc, AX.X, ALU.add))
                nc.vector.tensor_scalar(ymean[:, lo:hi], ysum[:, lo:hi], 1.0 / D, None, ALU.mult).then_inc(f_dve, 1)
                dve.wait_ge(f_dve, 3 * c + 2)
                nc.vector.tensor_tensor(yc, yc, ymean[:, lo:hi].unsqueeze(2).to_broadcast([P, CH, D]), ALU.subtract).then_inc(f_dve, 1)
                dve.wait_ge(f_sq, c + 1)
                nc.vector.tensor_reduce(yssq[:, lo:hi], y2c, AX.X, ALU.add).then_inc(f_ss, 1)
                dve.wait_ge(f_sd, c + 1)
                link(nc.vector.reciprocal(yrstd[:, lo:hi], ystd[:, lo:hi]))
                link(nc.vector.tensor_scalar(yrstd[:, lo:hi], yrstd[:, lo:hi], float(D) ** 0.5, None, ALU.mult))
                nc.vector.tensor_tensor(yc, yc, yrstd[:, lo:hi].unsqueeze(2).to_broadcast([P, CH, D]), ALU.mult).then_inc(f_y, 1)


_INS = ['x', 'src', 'dst', 'edge_attr_128', 'L0_gnn_W', 'L0_gnn_b', 'L0_gnn_gamma', 'L0_gnn_beta']
_OUTS = [((6250, 128), 'float32')]


def kernel(**inputs):
    import numpy as _np
    import concourse.bacc as _bacc
    from concourse import mybir as _mybir
    from concourse.bass_utils import run_bass_kernel_spmd as _run

    nc = _bacc.Bacc("TRN2", target_bir_lowering=False, num_devices=1)
    arrays, args = {}, []
    for name in _INS:
        a = _np.ascontiguousarray(inputs[name])
        arrays[f"in_{name}_dram"] = a
        args.append(nc.dram_tensor(f"in_{name}_dram", a.shape, _mybir.dt.from_np(a.dtype), kind="ExternalInput").ap())
    for i, (shape, dtype) in enumerate(_OUTS):
        dt = _mybir.dt.from_np(_np.dtype(dtype))
        args.append(nc.dram_tensor(f"out_{i}_dram", shape, dt, kind="ExternalOutput").ap())
    bass_gnn_resnorm(nc, *args)
    r = _run(nc, [arrays], core_ids=[0])
    got = tuple(r.results[0][f"out_{i}_dram"] for i in range(len(_OUTS)))
    return got[0]
```

```python
import concourse.bass as bass
from concourse import mybir
from contextlib import ExitStack

F32 = mybir.dt.float32
BF16 = mybir.dt.bfloat16
I32 = mybir.dt.int32
ALU = mybir.AluOpType
ACT = mybir.ActivationFunctionType
AX = mybir.AxisListType

P = 128
D = 128
LN_EPS = 1e-5
NG_COLS = 8
GE = P * NG_COLS
SUPER = 512
SJ = SUPER // P
ROW = D + 1
RING = 4
NODE_RING = 6


def bass_gnn_resnorm(nc, x, src, dst, edge, W, b, gamma, beta, out):
    N = x.shape[0]
    E = src.shape[0]
    NB = -(-N // P)
    N_LAST = N - (NB - 1) * P
    NG = -(-E // GE)
    OVER = NG * GE - E
    C = NG * NG_COLS
    BK = NB + 1
    NS = (E + NB * SUPER) // SUPER
    NS_ALL = NS + NODE_RING
    assert OVER % NG_COLS == 0 and NG % 2 == 0 and E % GE != 0

    TAIL = NODE_RING - 1
    MIN_TRIPS = NB // NODE_RING
    W_MAX = NB * P - P

    tabB = nc.dram_tensor("tabB", (NB * P, D), F32)
    rows = nc.dram_tensor("rows", ((NS_ALL + 1) * SUPER, ROW), F32)
    rows_ap = rows.ap()
    rows_quads = rows_ap.rearrange("(r j) c -> r (j c)", j=SJ)
    rows_super = rows_ap.rearrange("(s p j) c -> s p (j c)", p=P, j=SJ)
    tabB_v = tabB.ap().rearrange("(t p) d -> p t d", p=P)
    x_v = x[0:(NB - 1) * P, :].rearrange("(t p) d -> p t d", p=P)
    out_v = out[0:(NB - 1) * P, :].rearrange("(t p) d -> p t d", p=P)
    edge_groups = edge[0:(NG - 1) * GE, :].rearrange("(g p j) d -> g p (j d)", p=P, j=NG_COLS)
    edge_last = edge[E - GE:E, :].rearrange("(p j) d -> p (j d)", j=NG_COLS)

    ctx = ExitStack()
    with ctx:
        def sb(name, shape, dt=F32):
            return ctx.enter_context(nc.sbuf_tensor(name, shape, dt))

        def sem(name):
            return ctx.enter_context(nc.semaphore(name))

        def sems(name, n):
            return [sem(f"{name}{i}") for i in range(n)]

        bank = [ctx.enter_context(nc.psum_tensor(f"bank{i}", [P, 512], F32)) for i in range(8)]

        iota_row = sb("iota_row", [P, P])
        iota_col = sb("iota_col", [P, 1])
        iota_sup = sb("iota_sup", [P, NS_ALL])
        ident = sb("ident", [P, P])
        before = sb("before", [P, P], BF16)
        not_before = sb("not_before", [P, P], BF16)
        ones_bf = sb("ones_bf", [P, P], BF16)
        ones_row = sb("ones_row", [1, P])
        eps128 = sb("eps128", [P, 1])
        w_sb = sb("w_sb", [P, 3, D])
        w_mean = sb("w_mean", [P, 3])
        wc = sb("wc", [P, 3, D])
        vecs = sb("vecs", [P, 3, D])
        b_mean = sb("b_mean", [P, 1])
        bc = sb("bc", [P, D])
        neg_beta = sb("neg_beta", [P, D])
        gamma_s = sb("gamma_s", [P, D])
        gb = vecs[:, 1, :]
        beta_bc = vecs[:, 2, :]
        w_low = sb("w_low", [NG, 1])
        w_high = sb("w_high", [NG, 1])
        w_diag = sb("w_diag", [NG, NG + 1])
        w_bc = sb("w_bc", [P, NG + 1])
        w_i = sb("w_i", [1, NG + 1], I32)
        dst_rel = sb("dst_rel", [P, C])
        dst_i = sb("dst_i", [P, C], I32)
        hi_bf = sb("hi_bf", [P, C], BF16)
        lo_f = sb("lo_f", [P, C])
        onehot = sb("onehot", [P, BK, C], BF16)
        tot = sb("tot", [P, BK, NG_COLS])
        cum = sb("cum", [P, BK * NG_COLS])
        excl = sb("excl", [P, BK, NG_COLS])
        cnt = sb("cnt", [P, BK])
        cnt_i = sb("cnt_i", [P, BK], I32)
        nsup = sb("nsup", [P, BK])
        sup_end = sb("sup_end", [P, BK])
        sup_start = sb("sup_start", [P, BK])
        shift = sb("shift", [P, BK])
        base = sb("base", [P, BK, NG_COLS])
        start_col = sb("start_col", [BK, 1])
        reached = sb("reached", [BK, NS_ALL])
        ones_f = sb("ones_f", [P, P])
        trips_i = sb("trips_i", [1, 1], I32)
        blk = sb("blk", [P, NS_ALL])
        last_f = sb("last_f", [P, NB + TAIL])
        last_idx = sb("last_idx", [P, NB + TAIL], I32)
        blk_i = sb("blk_i", [1, NS_ALL], I32)
        trips = sb("trips", [1, 1], I32)
        fill = sb("fill", [P, SJ, ROW])
        x_last = sb("x_last", [P, D])
        xT = sb("xT", [P, 2, 512])
        tabA_sb = sb("tabA_sb", [P, NB, D])
        b_st = sb("b_st", [P, 4, 4, D])
        e_sb = sb("e_sb", [P, RING, GE])
        eT = sb("eT", [P, 2, 512])
        b_rows = sb("b_rows", [P, RING, NG_COLS, D])
        b_win = [b_rows[:, k, 0, :] for k in range(RING)]
        hot_d = b_rows[:, 0:2, 1:5, :]
        hot_dT = [b_rows[:, 2 + h, 1:5, :].rearrange("p t d -> p (t d)") for h in range(2)]
        stage_room = sb("stage_room", [P, RING * NG_COLS * ROW])
        stage = stage_room[:].rearrange("p (k j c) -> p k j c", k=RING, j=NG_COLS)
        prod = sb("prod", [P, BK, NG_COLS])
        pos_idx = sb("pos_idx", [P, RING, NG_COLS], I32)
        idx_rows = b_rows[0:NG, 0:2, :, :].rearrange("p v t d -> p v (t d)").bitcast(I32)
        x_third = [b_rows[:, h:h + 2, :, :].rearrange("p v t d -> p (v t) d") for h in (2, 0, 2)]
        idx_f = stage_room[0:NG, 0:2 * GE].rearrange("p (v e) -> p v e", v=2)
        src_i = eT[:].rearrange("p h e -> p (h e)")[:, 0:C].bitcast(I32)
        hi_i = dst_i
        lo_i = stage_room[:, 2 * GE:2 * GE + C].bitcast(I32)
        dst_idx = sb("dst_idx", [P, RING, NG_COLS], I32)
        hs = [stage_room[:, k * SJ * ROW:(k + 1) * SJ * ROW].rearrange("p (j c) -> p j c", j=SJ) for k in range(NODE_RING)]
        quads = [e_sb[:, k // 2, 512 * (k % 2):512 * (k % 2) + 512] for k in range(2 * RING)]
        sel = [q.rearrange("p (j n) -> p j n", j=SJ) for q in quads[0:NODE_RING]]
        selT = [xT[:, k, :] for k in range(2)]
        pre = [q.rearrange("p (j n) -> p j n", j=SJ) for q in quads[6:8]]
        msg_room = b_rows[:].rearrange("p k j d -> p (k j d)")[:, 0:NODE_RING * SJ * ROW].rearrange("p (k j c) -> p k j c", k=NODE_RING, j=SJ)
        msg = [msg_room[:, k, :, :] for k in range(NODE_RING)]
        SEL_AT = 3
        DVE_J = 2
        ssq = sb("ssq", [P, 2, SJ])
        std = sb("std", [P, 2, SJ])
        rstd = sb("rstd", [P, 2, SJ])
        CH = 7
        NCH = NB // CH
        ACT_CHUNKS = (2, 4)
        STD_LAG = 3
        assert NCH * CH == NB
        room = onehot[:].rearrange("p b c -> p (b c)").bitcast(F32)
        sums = room[:, 0:NB * ROW].rearrange("p (t c) -> p t c", t=NB)
        y = sums[:, :, 0:D]
        y2 = room[:, NB * ROW:NB * (ROW + D)].rearrange("p (t d) -> p t d", t=NB)
        eps = sb("eps", [P, 1])
        ystat = sb("ystat", [P, NB, 6])
        ymv = sb("ymv", [P, NB, 2])
        ystd = sb("ystd", [P, NB])
        yrstd = sb("yrstd", [P, NB])
        yshift = sb("yshift", [P, NB])

        s_iota = sem("iota_made")
        s_const = sem("constants_made")
        s_win = sem("windows_found")
        s_wbc = sem("windows_broadcast")
        w_ready = sems("b_window_loaded", RING)
        hd_made = sem("dst_selectors_made")
        hd_t = sem("dst_selectors_transposed")
        hd_c = sem("dst_selectors_copied")
        n_scaled = sem("gamma_multiplied")
        n_cnt = sem("count_columns_cleared")
        n_selp = sem("pool_selectors_made")
        s_idx_in = sem("src_loaded")
        s_dst_in = sem("dst_loaded")
        s_bias = sem("bias_centred")
        s_last = sem("last_supertiles_known")
        s_idx_f = sem("indices_as_float")
        s_idx_t = sem("indices_transposed")
        s_dve = sem("dve_chain")
        s_dst_col = sem("dst_columns_copied")
        s_hot = sem("onehot_made")
        s_cnt = sem("counts_summed")
        s_base = sem("bases_made")
        s_col = sem("starts_transposed")
        s_reach = sem("starts_compared")
        s_blk = sem("blocks_summed")
        s_tabs = sem("index_tables_made")
        s_fillv = sem("fill_rows_made")
        s_fill = sem("fills_landed")
        s_fill_sp = sem("sp_fills_landed")
        s_w = sem("weights_loaded")
        s_v = sem("vectors_loaded")
        s_wc = sem("weights_centred")
        s_xz = sem("last_block_cleared")
        s_x = sems("x_third_loaded", 3)
        s_xl = sem("last_block_loaded")
        s_xt = sem("x_transposed")
        s_xc = sem("xT_copied")
        s_ab = sem("tables_multiplied")
        s_ac = sem("tables_copied")
        s_bb = sem("bias_added")
        s_tab = sems("tables_stored", 4)
        s_turn = sem("pool_turns")
        e_ready = sems("e_loaded", RING)
        e_used = sem("e_transposed")
        eT_ready = sem("eT_copied")
        h_done = sem("edges_multiplied")
        rank_mm = sem("ranks_summed")
        rank_read = sem("ranks_read")
        pos_ready = sem("positions_made")
        dsti_ready = sem("dst_indices_made")
        b_ready = sems("b_rows_gathered", RING)
        lo_ready = sem("node_numbers_staged")
        st_ready = sem("rows_staged")
        st_free = sems("rows_scattered", RING)
        hs_ready = sems("hs_loaded", NODE_RING)
        y_head = sem("first_blocks_of_x_in_place")
        y_rest = sem("other_blocks_of_x_in_place")
        n_sel = sem("selectors_made")
        n_selT = sem("selectors_transposed")
        n_selTc = sem("selT_copied")
        n_a = sem("a_rows_selected")
        n_pre = sem("pre_made")
        n_ssq = sem("squares_summed")
        n_std = sem("std_made")
        n_msg = sem("messages_made")
        n_o = sem("messages_summed")
        n_run = sem("runs_made")
        n_rs = sem("rstd_made")
        tr_half = sem("e_first_half_transposed")
        f_eb = sem("edges_times_beta")
        f_add = sem("terms_added")
        f_st = sem("final_stats")
        f_mv = sem("final_mean_and_variance")
        f_sd = sem("final_std")
        f_sc = sem("final_scales")
        f_ya = sem("act_final_rows")
        f_yd = sem("dve_final_rows")
        f_out = sem("output_stored")

        NQ = (NB - 1) // 4
        NIT = NG // RING
        LAST = NG - NIT * RING
        CNT = 7
        EARLY = 4
        SP_FILLS = 2
        SP_EARLY = (NQ - EARLY) * SP_FILLS
        SP_LATE = 3
        assert (NB - 1) % NODE_RING == 0 and (NB - 1) // NODE_RING >= NODE_RING
        assert NQ * 4 == NB - 1 and NQ % 3 == 0 and NG % (2 * CNT) == 0
        DIV_SHIFT = 15
        DIV_MULT = -(-(1 << DIV_SHIFT) // NODE_RING)
        assert NS_ALL * DIV_MULT < 1 << 24
        assert all(n * DIV_MULT >> DIV_SHIFT == n // NODE_RING for n in range(NS_ALL + 1))
        TQ = NQ // 3

        def x_blocks(q, t):
            return x_third[q // TQ][:, (q % TQ) * 4 + t, :]

        def zeroth(g):
            return isinstance(g, int) and g == 0

        def below(n, d, lim):
            return isinstance(n, int) and n + d < lim

        def group_trips(eng, step):
            for k in range(RING):
                step(k, k, 0)
            with eng.Fori(1, NIT) as i:
                for k in range(RING):
                    step(i * RING + k, k, i)
            for k in range(LAST):
                step(NIT * RING + k, k, NIT)

        def super_trips(eng, n_trips, step):
            for n in range(-4, NODE_RING):
                step(n, n % NODE_RING, n // NODE_RING, lambda lag, n=n: n + lag >= 0)
            with eng.Fori(1, n_trips - 1) as i:
                for k in range(NODE_RING):
                    step(i * NODE_RING + k, k, i, lambda lag: True)
            for t in range(-NODE_RING, 3):
                k = t % NODE_RING
                step(n_trips * NODE_RING + t, k, n_trips + t // NODE_RING, lambda lag, t=t: t + lag < 0)

        def groups_without_window(eng):
            wide = eng.alloc_register("wide_groups")
            eng.reg_load(wide, w_i[0:1, NG:NG + 1])
            return wide

        def trip_count(eng):
            return eng.value_load(trips[0:1, 0:1], min_val=0, max_val=NS_ALL // NODE_RING - MIN_TRIPS) + MIN_TRIPS

        block = ctx.enter_context(nc.Block())

        @block.sync
        def _(sp):
            sp.dma_start(idx_rows[0:NG - 2, 0, :], src[0:(NG - 2) * GE].rearrange("(g e) -> g e", e=GE)).then_inc(s_idx_in, 16)
            sp.dma_start(idx_rows[NG - 2:NG - 1, 0, :], src[(NG - 2) * GE:(NG - 1) * GE].rearrange("(g e) -> g e", g=1)).then_inc(s_idx_in, 16)
            sp.dma_start(idx_rows[NG - 1:NG, 0, :], src[E - GE:E].rearrange("(g e) -> g e", g=1)).then_inc(s_idx_in, 16)
            sp.dma_start(w_sb[:], W.rearrange("(t p) d -> p t d", p=P)).then_inc(s_w, 16)

            def load_third(i):
                sp.dma_start(x_third[i], x_v[:, i * 4 * TQ:(i + 1) * 4 * TQ, :]).then_inc(s_x[i], 16)

            load_third(0)
            sp.wait_ge(s_xz, 1)
            sp.dma_start(x_last[0:N_LAST, :], x[(NB - 1) * P:N, :]).then_inc(s_xl, 16)
            sp.wait_ge(s_idx_f, 2)
            load_third(1)

            def load_edges(g, k):
                if not below(g, 0, RING):
                    sp.wait_ge(e_used, g - RING + 1)
                last = isinstance(g, int) and g == NG - 1
                sp.dma_start(e_sb[:, k, :], edge_last if last else edge_groups[g]).then_inc(e_ready[k], 16)

            for k in range(RING):
                load_edges(k, k)
            def store(q, nblk=4):
                k = q % 4
                rows_of = bass.ds(q * 4, nblk)
                sp.wait_ge(s_bb, q + 1)
                sp.dma_start(tabB_v[:, rows_of, :], b_st[:, k, 0:nblk, :]).then_inc(s_tab[k], 16)

            fill_rows = fill[:].rearrange("p j c -> p (j c)")

            def fill_supertiles(first, n):
                for t in range(first, first + n):
                    at = sp.value_load(last_idx[0:1, t:t + 1], min_val=0, max_val=(NS_ALL - 1) * P)
                    sp.dma_start(rows_quads[bass.ds(at, P), :], fill_rows).then_inc(s_fill_sp, 16)

            for q in range(NQ):
                store(q)
                if q == 0:
                    sp.wait_ge(s_xt, TQ)
                    load_third(2)
                if q == EARLY:
                    sp.wait_ge(s_last, 1)
                    sp.wait_ge(s_fillv, 2)
                if q >= EARLY:
                    fill_supertiles((q - EARLY) * SP_FILLS, SP_FILLS)
            store(NQ, 1)
            for k in range(4):
                sp.wait_ge(s_tab[k], 16 * (NQ // 4 + (k == 0)))
            sp.wait_ge(s_tabs, 1)

            with sp.If_eq(groups_without_window(sp), 0):
                def load_window(g, k):
                    if not below(g, 0, RING):
                        sp.wait_ge(h_done, 2 * (g - RING) + 2)
                    at = sp.value_load(w_i[0:1, bass.ds(g, 1)], min_val=0, max_val=W_MAX)
                    sp.dma_start(b_win[k], tabB.ap()[bass.ds(at, P), :]).then_inc(w_ready[k], 16)

                for k in range(RING):
                    load_window(k, k)
                fill_supertiles(SP_EARLY, SP_LATE)

                def step(g, k, u):
                    if not below(g, 0, RING):
                        load_edges(g, k)
                        load_window(g, k)
                group_trips(sp, step)
            with sp.Else():
                fill_supertiles(SP_EARLY, SP_LATE)

                def step(g, k, u):
                    if not below(g, 0, RING):
                        load_edges(g, k)
                group_trips(sp, step)

            n_trips = trip_count(sp)
            for k in range(RING):
                sp.wait_ge(st_free[k], 16 * NG_COLS * (NIT + (k < LAST)))

            def step(n, k, i, on):
                if on(4):
                    s, kk = n + 4, (k + 4) % NODE_RING
                    if not below(n, 4, NODE_RING):
                        sp.wait_ge(n_pre, s - NODE_RING + 1)
                    sp.dma_start(hs[kk], rows_super[s]).then_inc(hs_ready[kk], 16)
                if isinstance(n, int) and n >= 0:
                    part = (NB - 1) // NODE_RING
                    sp.dma_start(y[:, n * part:(n + 1) * part, :], x_v[:, n * part:(n + 1) * part, :]).then_inc(
                        y_rest if n else y_head, 16)
            super_trips(sp, n_trips, step)

            for c in range(NCH):
                lo, hi = c * CH, (c + 1) * CH
                by_act = sum(a <= c for a in ACT_CHUNKS)
                if c in ACT_CHUNKS:
                    sp.wait_ge(f_ya, by_act)
                else:
                    sp.wait_ge(f_yd, c + 1 - by_act)
                if c < NCH - 1:
                    sp.dma_start(out_v[:, lo:hi, :], y2[:, lo:hi, :]).then_inc(f_out, 16)
                else:
                    sp.dma_start(out_v[:, lo:hi - 1, :], y2[:, lo:hi - 1, :]).then_inc(f_out, 16)
                    sp.dma_start(out[(NB - 1) * P:N, :], y2[0:N_LAST, hi - 1, :]).then_inc(f_out, 16)
            sp.wait_ge(f_out, 16 * (NCH + 1))

        @block.gpsimd
        def _(pool):
            nc.gpsimd.iota(iota_row[:], [[1, P]], base=0, channel_multiplier=0,
                           allow_small_or_imprecise_dtypes=True).then_inc(s_iota, 1)
            nc.gpsimd.iota(iota_col[:], [[0, 1]], base=0, channel_multiplier=1,
                           allow_small_or_imprecise_dtypes=True).then_inc(s_iota, 1)
            nc.gpsimd.iota(iota_sup[:], [[1, NS_ALL]], base=0, channel_multiplier=0,
                           allow_small_or_imprecise_dtypes=True).then_inc(s_iota, 1)
            nc.gpsimd.memset(x_last[:], 0.0).then_inc(s_xz, 1)
            nc.gpsimd.memset(ones_bf[:], 1.0).then_inc(s_const, 1)
            nc.gpsimd.memset(ones_row[:], 1.0).then_inc(s_const, 1)
            nc.gpsimd.memset(ones_f[:], 1.0).then_inc(s_const, 1)
            nc.gpsimd.memset(eps128[:], D * LN_EPS).then_inc(s_const, 1)
            nc.gpsimd.memset(eps[:], LN_EPS).then_inc(s_const, 1)
            nc.gpsimd.memset(fill[:], 0.0).then_inc(s_fillv, 1)
            pool.wait_ge(s_fillv, 1)
            nc.gpsimd.memset(fill[:, :, D:ROW], -1.0).then_inc(s_fillv, 1)

            def settle():
                pool.sem_inc(s_turn, 1)

            pool.wait_ge(s_bias, 1)
            for q in range(EARLY):
                pool.wait_ge(s_ac, 2 * q + 2)
                nc.gpsimd.tensor_tensor(b_st[:, q % 4, :, :], b_st[:, q % 4, :, :], bc[:].unsqueeze(1).to_broadcast([P, 4, D]),
                                        ALU.add).then_inc(s_bb, 1)

            pool.wait_ge(s_last, 1)
            pool.wait_ge(s_fillv, 2)
            fill_rows = fill[:].rearrange("p j c -> p (j c)")
            pool_fills = list(range(SP_EARLY + SP_LATE, NB + TAIL))
            for t in pool_fills:
                nc.gpsimd.indirect_dma_start(rows_quads, bass.IndirectOffsetOnAxis(last_idx[:, t:t + 1], 0),
                                             fill_rows, None).then_inc(s_fill, 16)

            pool.wait_ge(s_tabs, 1)
            pool.wait_ge(s_fill, 16 * len(pool_fills))
            pool.wait_ge(s_fill_sp, 16 * (SP_EARLY + SP_LATE))

            def scatter(g, k):
                pool.wait_ge(pos_ready, g + 1)
                pool.wait_ge(lo_ready, g + 1)
                pool.wait_ge(st_ready, 2 * g + 2)
                settle()
                for j in range(NG_COLS):
                    nc.gpsimd.indirect_dma_start(rows_ap, bass.IndirectOffsetOnAxis(pos_idx[:, k, j:j + 1], 0),
                                                 stage[:, k, j, :], None).then_inc(st_free[k], 16)

            with pool.If_eq(groups_without_window(pool), 0):
                group_trips(pool, lambda g, k, u: scatter(g, k))
            with pool.Else():
                for k in range(4):
                    pool.wait_ge(s_tab[k], 16 * (NQ // 4 + (k == 0)))

                def gather_b(g, k):
                    pool.wait_ge(dsti_ready, g + 1)
                    if not below(g, 0, RING):
                        pool.wait_ge(st_ready, 2 * (g - RING) + 2)
                    settle()
                    for j in range(NG_COLS):
                        nc.gpsimd.indirect_dma_start(b_rows[:, k, j, :], None, tabB.ap(),
                                                     bass.IndirectOffsetOnAxis(dst_idx[:, k, j:j + 1], 0)).then_inc(b_ready[k], 16)

                def step(g, k, u):
                    if not (isinstance(g, int) and g + 2 >= NG):
                        gather_b(g + 2, (k + 2) % RING)
                    scatter(g, k)
                gather_b(0, 0)
                gather_b(1, 1)
                group_trips(pool, step)

            n_trips = trip_count(pool)

            def step(n, k, i, on):
                if on(2):
                    s, kk = n + 2, (k + 2) % NODE_RING
                    pool.wait_ge(hs_ready[kk], (i + (k + 2) // NODE_RING) * 16 + 16)
                    if not below(n, 2, NODE_RING):
                        pool.wait_ge(n_o, s - NODE_RING + 1)
                    settle()
                    for j in range(DVE_J, SJ):
                        a = nc.gpsimd.tensor_scalar(sel[kk][:, j, :], iota_row[:], hs[kk][:, j, D:ROW], None, ALU.is_equal)
                    a.then_inc(n_selp, 1)
                if on(0):
                    s = n
                    pool.wait_ge(n_pre, s + 1)
                    if not below(n, 0, NODE_RING):
                        pool.wait_ge(n_o, s - NODE_RING + 1)
                    nc.gpsimd.tensor_tensor(msg[k][:, :, 0:D], pre[k % 2], gamma_s[:].unsqueeze(1).to_broadcast([P, SJ, D]),
                                            ALU.mult).then_inc(n_scaled, 1)
            super_trips(pool, n_trips, step)

            for c in range(NCH):
                pool.wait_ge(f_eb, c + 1)
                yc = y[:, c * CH:(c + 1) * CH, :]
                nc.gpsimd.tensor_tensor(yc, yc, y2[:, c * CH:(c + 1) * CH, :], ALU.add).then_inc(f_add, 1)

        @block.tensor
        def _(pe):
            pe.wait_ge(s_const, 6)
            for v in range(2):
                pe.wait_ge(s_idx_f, v + 1)
                for j in range(NG_COLS):
                    o = bank[2 * v + j // 4][:, 0:4 * NG].rearrange("p (j g) -> p j g", j=4)
                    mm = pe.transpose(o[:, j % 4, :], idx_f[:, v, j::NG_COLS], ident[0:NG, 0:NG])
                mm.then_inc(s_idx_t, 1)

            def x_turn(q, nblk=4):
                if q < NQ and q % TQ == 0:
                    pe.wait_ge(s_x[q // TQ], 16)
                if q == NQ:
                    pe.wait_ge(s_xl, 16)
                if q >= 2:
                    pe.wait_ge(s_xc, q - 1)
                for t in range(nblk):
                    mm = pe.transpose(bank[4 + q % 2][:, t * P:(t + 1) * P], x_last[:] if q == NQ else x_blocks(q, t), ident[:])
                mm.then_inc(s_xt, 1)

            def x_mult(q, nblk=4):
                pe.wait_ge(s_xc, q + 1)
                if q >= 2:
                    pe.wait_ge(s_ac, 2 * q - 2)
                for t in range(nblk):
                    mm = pe.matmul(bank[(6, 2)[q % 2] + t // 2][:, (t % 2) * 256:(t % 2) * 256 + 256],
                                   xT[:, q % 2, t * P:(t + 1) * P], wc[:, 0:2, :].rearrange("p t d -> p (t d)"),
                                   start=True, stop=True)
                mm.then_inc(s_ab, 1)

            x_turn(0)
            pe.wait_ge(s_wc, 1)
            for q in range(EARLY):
                x_turn(q + 1)
                if q == 1:
                    pe.wait_ge(s_dst_col, 1)
                x_mult(q)

            def hot(g):
                return onehot[:, :, bass.ds(g * NG_COLS, NG_COLS)]

            total = bank[0][:, 0:BK * NG_COLS].rearrange("p (b j) -> p b j", j=NG_COLS)
            pe.wait_ge(s_hot, 1)
            for g in range(CNT):
                pe.matmul(total, ones_bf[:], hot(g), start=(g == 0), stop=False)
            with pe.Fori(1, NG // CNT // 2) as i:
                for g in range(CNT):
                    pe.matmul(total, ones_bf[:], hot(i * CNT + g), start=False, stop=False)
            pe.wait_ge(s_hot, 2)
            with pe.Fori(NG // CNT // 2, NG // CNT - 1) as i:
                for g in range(CNT):
                    pe.matmul(total, ones_bf[:], hot(i * CNT + g), start=False, stop=False)
            for g in range(NG - CNT, NG):
                mm = pe.matmul(total, ones_bf[:], hot(g), start=False, stop=(g == NG - 1))
            mm.then_inc(s_cnt, 1)
            pe.wait_ge(s_win, 1)
            pe.matmul(bank[1][:, 0:NG + 1], ones_f[0:NG, :], w_diag[:], start=True, stop=True).then_inc(s_wbc, 1)

            for q in range(EARLY, NQ):
                x_turn(q + 1, 4 if q + 1 < NQ else 1)
                x_mult(q)
                if q == EARLY:
                    pe.wait_ge(s_base, 1)
                    pe.transpose(bank[0][0:BK, 0:P], sup_start[:], ident[:]).then_inc(s_col, 1)
                if q == EARLY + 1:
                    pe.wait_ge(s_reach, 1)
                    pe.matmul(bank[0][:, P:P + NS_ALL], ones_f[0:NB, :], reached[0:NB, :], start=True, stop=True).then_inc(s_blk, 1)
            x_mult(NQ, 1)

            acc = bank[1][:, 0:BK * NG_COLS].rearrange("p (b j) -> p b j", j=NG_COLS)
            pe.wait_ge(s_tabs, 1)
            pe.matmul(bank[1][:, 0:BK * NG_COLS], ones_row[:], base[0:1, :, :].rearrange("p b j -> p (b j)"),
                      start=True, stop=False, skip_group_check=True)
            pe.wait_ge(s_ac, 2 * NQ + 1)

            def ranks(g):
                if not zeroth(g):
                    pe.wait_ge(rank_read, g)
                    pe.matmul(acc, not_before[:], hot(g - 1), start=False, stop=False, skip_group_check=True)
                pe.matmul(acc, before[:], hot(g), start=False, stop=True, skip_group_check=True).then_inc(rank_mm, 1)

            def turn_edges(g, k, u):
                pe.wait_ge(e_ready[k], u * 16 + 16)
                for h in range(2):
                    if not zeroth(g):
                        pe.wait_ge(eT_ready, 2 * g + h - 1)
                    for t in range(4):
                        j = 4 * h + t
                        mm = pe.transpose(bank[4 + h][:, t * P:(t + 1) * P], e_sb[:, k, j * D:(j + 1) * D], ident[:])
                    mm.then_inc((tr_half, e_used)[h], 1)

            with pe.If_eq(groups_without_window(pe), 0):
                def step(g, k, u):
                    for h in range(2):
                        pe.wait_ge(hd_made, 2 * g + h + 1)
                        if not zeroth(g):
                            pe.wait_ge(hd_c, 2 * g + h - 1)
                        for t in range(4):
                            mm = pe.transpose(bank[2 + h][:, t * P:(t + 1) * P], hot_d[:, h, t, :], ident[:])
                        mm.then_inc(hd_t, 1)
                    turn_edges(g, k, u)
                    ranks(g)
                    pe.wait_ge(w_ready[k], u * 16 + 16)
                    for h in range(2):
                        pe.wait_ge(hd_c, 2 * g + h + 1)
                        pe.wait_ge(eT_ready, 2 * g + h + 1)
                        if not zeroth(g):
                            pe.wait_ge(st_ready, 2 * g + h - 1)
                        for t in range(4):
                            pe.matmul(bank[6 + h][:, t * D:(t + 1) * D], eT[:, h, t * P:(t + 1) * P], wc[:, 2, :],
                                      start=True, stop=False)
                            mm = pe.matmul(bank[6 + h][:, t * D:(t + 1) * D], hot_dT[h][:, t * P:(t + 1) * P], b_win[k],
                                           start=False, stop=True)
                        mm.then_inc(h_done, 1)
                group_trips(pe, step)
            with pe.Else():
                def step(g, k, u):
                    ranks(g)
                    turn_edges(g, k, u)
                    for h in range(2):
                        pe.wait_ge(eT_ready, 2 * g + h + 1)
                        if not zeroth(g):
                            pe.wait_ge(st_ready, 2 * g + h - 1)
                        for t in range(4):
                            mm = pe.matmul(bank[6 + h][:, t * D:(t + 1) * D], eT[:, h, t * P:(t + 1) * P], wc[:, 2, :],
                                           start=True, stop=True)
                        mm.then_inc(h_done, 1)
                group_trips(pe, step)

            def step(n, k, i, on):
                if on(1):
                    s, b2 = n + 1, (k + 1) % 2
                    at = pe.value_load(blk_i[0:1, bass.ds(s, 1)], min_val=0, max_val=NB - 1)
                    pe.wait_ge(n_sel, s + 1)
                    pe.wait_ge(n_selp, s + 1)
                    if not below(n, 1, 2):
                        pe.wait_ge(n_selTc, s - 1)
                    for j in range(SJ):
                        mm = pe.transpose(bank[b2][:, j * P:(j + 1) * P], sel[(k + 1) % NODE_RING][:, j, :], ident[:])
                    mm.then_inc(n_selT, 1)
                if on(-2):
                    s, b2 = n - 2, k % 2
                    pe.wait_ge(n_msg, s + 1)
                    if not below(n, -2, 3):
                        pe.wait_ge(n_run, s - 2)
                    for j in range(SJ):
                        mm = pe.matmul(bank[4 + (k - 2) % 3][:, 0:ROW], sel[(k - 2) % NODE_RING][:, j, :], msg[(k - 2) % NODE_RING][:, j, :],
                                       start=(j == 0), stop=(j == SJ - 1))
                    mm.then_inc(n_o, 1)
                if on(1):
                    s, b2 = n + 1, (k + 1) % 2
                    pe.wait_ge(n_selTc, s + 1)
                    if not below(n, 1, 2):
                        pe.wait_ge(n_pre, s - 1)
                    for j in range(SJ):
                        mm = pe.matmul(bank[2 + b2][:, j * D:(j + 1) * D], selT[b2][:, j * P:(j + 1) * P], tabA_sb[:, bass.ds(at, 1), :],
                                       start=True, stop=True)
                    mm.then_inc(n_a, 1)
            super_trips(pe, trip_count(pe), step)

        @block.scalar
        def _(act):
            act.dma_start(idx_rows[0:NG - 2, 1, :], dst[0:(NG - 2) * GE].rearrange("(g e) -> g e", e=GE)).then_inc(s_dst_in, 16)
            act.dma_start(idx_rows[NG - 2:NG - 1, 1, :], dst[(NG - 2) * GE:(NG - 1) * GE].rearrange("(g e) -> g e", g=1)).then_inc(s_dst_in, 16)
            act.dma_start(idx_rows[NG - 1:NG, 1, :], dst[E - GE:E].rearrange("(g e) -> g e", g=1)).then_inc(s_dst_in, 16)
            for n, v in enumerate((b, gamma, beta)):
                act.dma_start(vecs[:, n, :], v.partition_broadcast(P)).then_inc(s_v, 16)

            def x_copy(q, nblk=4):
                act.wait_ge(s_xt, q + 1)
                if q >= 2:
                    act.wait_ge(s_ab, q - 1)
                nc.scalar.copy(xT[:, q % 2, 0:nblk * P], bank[4 + q % 2][:, 0:nblk * P]).then_inc(s_xc, 1)

            def ab_copy(q, nblk=4):
                act.wait_ge(s_ab, q + 1)
                if q >= 4:
                    act.wait_ge(s_tab[q % 4], 16 * (q // 4))
                for h in range(-(-nblk // 2)):
                    m = min(2, nblk)
                    o = bank[(6, 2)[q % 2] + h][:, 0:m * 256].rearrange("p (t w d) -> p t w d", t=m, w=2)
                    nc.scalar.copy(tabA_sb[:, 4 * q + 2 * h:4 * q + 2 * h + m, :], o[:, :, 0, :])
                    nc.scalar.copy(b_st[:, q % 4, 2 * h:2 * h + m, :], o[:, :, 1, :]).then_inc(s_ac, 1)

            x_copy(0)
            for q in range(NQ):
                x_copy(q + 1, 4 if q + 1 < NQ else 1)
                ab_copy(q)
            ab_copy(NQ, 1)

            act.wait_ge(s_tabs, 1)

            def number_rows(g, k, u):
                if not below(g, 0, RING):
                    act.wait_ge(st_free[k], u * 16 * NG_COLS)
                nc.scalar.copy(stage[:, k, :, D], lo_f[:, bass.ds(g * NG_COLS, NG_COLS)]).then_inc(lo_ready, 1)

            def copy_edges(g, k, u):
                for h in range(2):
                    act.wait_ge((tr_half, e_used)[h], g + 1)
                    if not zeroth(g):
                        act.wait_ge(h_done, 2 * g + h - 1)
                    nc.scalar.copy(eT[:, h, :], bank[4 + h][:]).then_inc(eT_ready, 1)

            with act.If_eq(groups_without_window(act), 0):
                def step(g, k, u):
                    for h in range(2):
                        act.wait_ge(hd_t, 2 * g + h + 1)
                        if not zeroth(g):
                            act.wait_ge(h_done, 2 * g + h - 1)
                        nc.scalar.copy(hot_dT[h], bank[2 + h][:]).then_inc(hd_c, 1)
                    copy_edges(g, k, u)
                    number_rows(g, k, u)
                    for h in range(2):
                        act.wait_ge(h_done, 2 * g + h + 1)
                        nc.scalar.copy(stage[:, k, 4 * h:4 * h + 4, 0:D],
                                       bank[6 + h][:].rearrange("p (t d) -> p t d", t=4)).then_inc(st_ready, 1)
                group_trips(act, step)
            with act.Else():
                def step(g, k, u):
                    copy_edges(g, k, u)
                    number_rows(g, k, u)
                group_trips(act, step)

            def step(n, k, i, on):
                if on(1):
                    s, b2 = n + 1, (k + 1) % 2
                    act.wait_ge(n_selT, s + 1)
                    if not below(n, 1, 2):
                        act.wait_ge(n_a, s - 1)
                    nc.scalar.copy(selT[b2], bank[b2][:]).then_inc(n_selTc, 1)
                if on(0):
                    s, b2 = n, k % 2
                    act.wait_ge(n_pre, s + 1)
                    if not below(n, 0, 2):
                        act.wait_ge(n_std, s - 1)
                    for j in range(SJ):
                        a = nc.scalar.activation(eT[:, b2, j * D:(j + 1) * D], pre[b2][:, j, :], ACT.Square,
                                                 accum_out=ssq[:, b2, j:j + 1])
                    a.then_inc(n_ssq, 1)
                    act.wait_ge(n_ssq, s + 1)
                    if not below(n, 0, 2):
                        act.wait_ge(n_rs, s - 1)
                    nc.scalar.activation(std[:, b2, :], ssq[:, b2, :], ACT.Sqrt, bias=eps128[:]).then_inc(n_std, 1)
            super_trips(act, trip_count(act), step)

            act.wait_ge(n_run, trip_count(act) * NODE_RING)
            for c in range(NCH + STD_LAG):
                if c < NCH:
                    for t in range(c * CH, (c + 1) * CH):
                        a = nc.scalar.activation(y2[:, t, :], beta_bc, ACT.Copy, scale=sums[:, t, D:ROW])
                    a.then_inc(f_eb, 1)
                d = c - STD_LAG
                if d >= 0:
                    act.wait_ge(f_mv, d + 1)
                    lo, hi = d * CH, (d + 1) * CH
                    nc.scalar.activation(ystd[:, lo:hi], ymv[:, lo:hi, 1], ACT.Sqrt, bias=eps[:]).then_inc(f_sd, 1)
                if d - 1 in ACT_CHUNKS:
                    act.wait_ge(f_sc, d)
                    for t in range((d - 1) * CH, d * CH):
                        a = nc.scalar.activation(y2[:, t, :], y[:, t, :], ACT.Identity, bias=yshift[:, t:t + 1],
                                                 scale=yrstd[:, t:t + 1])
                    a.then_inc(f_ya, 1)

        @block.vector
        def _(dve):
            chain = [0]

            def link(ins):
                chain[0] += 1
                ins.then_inc(s_dve, 1)
                dve.wait_ge(s_dve, chain[0])

            dve.wait_ge(s_iota, 3)
            nc.vector.tensor_scalar(ident[:], iota_row[:], iota_col[:], None, ALU.is_equal).then_inc(s_const, 1)
            nc.vector.tensor_scalar(before[:], iota_row[:], iota_col[:], None, ALU.is_gt)
            nc.vector.tensor_scalar(not_before[:], iota_row[:], iota_col[:], None, ALU.is_le)
            dve.wait_ge(s_idx_in, 48)
            nc.vector.tensor_copy(idx_f[:, 0, :], idx_rows[:, 0, :]).then_inc(s_idx_f, 1)
            dve.wait_ge(s_dst_in, 48)
            nc.vector.tensor_copy(idx_f[:, 1, :], idx_rows[:, 1, :]).then_inc(s_idx_f, 1)
            dve.wait_ge(s_w, 16)
            link(nc.vector.tensor_reduce(w_mean[:], w_sb[:], AX.X, ALU.add))
            link(nc.vector.tensor_scalar(w_mean[:], w_mean[:], 1.0 / D, None, ALU.mult))
            nc.vector.tensor_tensor(wc[:], w_sb[:], w_mean[:].unsqueeze(2).to_broadcast([P, 3, D]), ALU.subtract).then_inc(s_wc, 1)
            dve.wait_ge(s_idx_t, 1)
            for h in range(2):
                o = src_i.rearrange("p (g j) -> p j g", j=NG_COLS)[:, 4 * h:4 * h + 4, :]
                a = nc.vector.tensor_copy(o, bank[h][:, 0:4 * NG].rearrange("p (j g) -> p j g", j=4))
            link(a)
            dve.wait_ge(s_idx_t, 2)
            for h in range(2):
                o = dst_rel[:].rearrange("p (g j) -> p j g", j=NG_COLS)[:, 4 * h:4 * h + 4, :]
                a = nc.vector.tensor_copy(o, bank[2 + h][:, 0:4 * NG].rearrange("p (j g) -> p j g", j=4))
            a.then_inc(s_dst_col, 1)
            nc.vector.tensor_scalar(hi_i[:], src_i, 7, None, ALU.logical_shift_right)
            link(nc.vector.tensor_scalar(lo_i, src_i, P - 1, None, ALU.bitwise_and))
            link(nc.vector.tensor_copy(hi_bf[:], hi_i[:]))
            link(nc.vector.memset(hi_bf[0:OVER // NG_COLS, C - NG_COLS:C], float(NB)))
            for h in range(2):
                half = slice(h * C // 2, (h + 1) * C // 2)
                for bk in range(BK):
                    a = nc.vector.tensor_scalar(onehot[:, bk, half], hi_bf[:, half], float(bk), None, ALU.is_equal)
                a.then_inc(s_hot, 1)
            dve.wait_ge(s_v, 48)
            link(nc.vector.tensor_reduce(b_mean[:], vecs[:, 0, :], AX.X, ALU.add))
            link(nc.vector.tensor_scalar(b_mean[:], b_mean[:], 1.0 / D, None, ALU.mult))
            nc.vector.tensor_scalar(bc[:], vecs[:, 0, :], b_mean[:], None, ALU.subtract).then_inc(s_bias, 1)
            nc.vector.tensor_scalar(neg_beta[:], beta_bc, -1.0, None, ALU.mult)
            nc.vector.tensor_scalar(gamma_s[:], gb, float(D) ** 0.5, None, ALU.mult)
            nc.vector.tensor_reduce(w_high[:], idx_f[:, 1, :], AX.X, ALU.max)
            link(nc.vector.tensor_reduce(w_low[:], idx_f[:, 1, :], AX.X, ALU.min))
            link(nc.vector.tensor_scalar(w_low[:], w_low[:], float(W_MAX), None, ALU.min))
            nc.vector.tensor_scalar(w_diag[:, 0:NG], ident[0:NG, 0:NG], w_low[:], None, ALU.mult)
            nc.vector.tensor_scalar(w_diag[:, NG:NG + 1], w_high[:], w_low[:], float(P - 1), ALU.subtract, ALU.is_gt).then_inc(s_win, 1)
            nc.vector.tensor_copy(lo_f[:], lo_i)
            link(nc.vector.tensor_copy(dst_i[:], dst_rel[:]))
            nc.vector.tensor_copy(dst_idx[:, 0, :], dst_i[:, 0:NG_COLS]).then_inc(dsti_ready, 1)
            nc.vector.tensor_copy(dst_idx[:, 1, :], dst_i[:, NG_COLS:2 * NG_COLS]).then_inc(dsti_ready, 1)
            dve.wait_ge(s_wbc, 1)
            nc.vector.tensor_copy(w_i[:], bank[1][0:1, 0:NG + 1])
            link(nc.vector.tensor_copy(w_bc[:], bank[1][:, 0:NG + 1]))
            dv = dst_rel[:].rearrange("p (g j) -> p g j", j=NG_COLS)
            nc.vector.tensor_tensor(dv, dv, w_bc[:, 0:NG].unsqueeze(2).to_broadcast([P, NG, NG_COLS]), ALU.subtract)

            dve.wait_ge(s_cnt, 1)
            link(nc.vector.tensor_copy(tot[:].rearrange("p b j -> p (b j)"), bank[0][:, 0:BK * NG_COLS]))
            link(nc.vector.tensor_reduce(cnt[:], tot[:], AX.X, ALU.add))
            link(nc.vector.tensor_scalar(cnt_i[:], cnt[:], float(SUPER - 1), None, ALU.add))
            link(nc.vector.tensor_scalar(cnt_i[:], cnt_i[:], 9, None, ALU.logical_shift_right))
            link(nc.vector.tensor_scalar(nsup[:], cnt_i[:], 1.0, None, ALU.max))
            link(nc.vector.tensor_tensor_scan(sup_end[:], nsup[:], nsup[:], 0.0, ALU.add, ALU.bypass))
            link(nc.vector.tensor_tensor(sup_start[:], sup_end[:], nsup[:], ALU.subtract))
            link(nc.vector.memset(sup_start[:, NB:BK], float(NS_ALL)))
            nc.vector.tensor_scalar(last_f[:, 0:NB], sup_end[:, 0:NB], -1.0, float(P), ALU.add, ALU.mult)
            link(nc.vector.tensor_scalar(last_f[:, NB:NB + TAIL], iota_sup[:, 0:TAIL], sup_end[:, NB - 1:NB], float(P), ALU.add, ALU.mult))
            nc.vector.tensor_scalar(last_idx[:], last_f[:], iota_col[:], None, ALU.add).then_inc(s_last, 1)
            totf = tot[:].rearrange("p b j -> p (b j)")
            link(nc.vector.tensor_tensor_scan(cum[:], totf, totf, 0.0, ALU.add, ALU.bypass))
            link(nc.vector.tensor_tensor(excl[:].rearrange("p b j -> p (b j)"), cum[:], totf, ALU.subtract))
            link(nc.vector.scalar_tensor_tensor(shift[:], sup_start[:], float(SUPER), excl[:, :, 0], ALU.mult, ALU.subtract))
            nc.vector.tensor_tensor(base[:], excl[:], shift[:].unsqueeze(2).to_broadcast([P, BK, NG_COLS]), ALU.add).then_inc(s_base, 1)
            link(nc.vector.tensor_scalar(trips_i[:], sup_end[0:1, NB - 1:NB], float(NODE_RING - 1), None, ALU.add))
            link(nc.vector.tensor_scalar(trips_i[:], trips_i[:], float(DIV_MULT), None, ALU.mult))
            link(nc.vector.tensor_scalar(trips_i[:], trips_i[:], DIV_SHIFT, None, ALU.logical_shift_right))
            nc.vector.tensor_scalar(trips[:], trips_i[:], float(-MIN_TRIPS), None, ALU.add)
            dve.wait_ge(s_col, 1)
            link(nc.vector.tensor_copy(start_col[:], bank[0][0:BK, 0:1]))
            nc.vector.tensor_scalar(reached[:], iota_sup[0:BK, :], start_col[:], None, ALU.is_ge).then_inc(s_reach, 1)
            dve.wait_ge(s_blk, 1)
            link(nc.vector.tensor_scalar(blk[:], bank[0][:, P:P + NS_ALL], -1.0, None, ALU.add))
            link(nc.vector.tensor_copy(blk_i[:], blk[0:1, :]))
            nc.vector.memset(ssq[:], 1.0).then_inc(s_tabs, 1)

            for q in range(EARLY, NQ + 1):
                nblk = 4 if q < NQ else 1
                dve.wait_ge(s_ac, 2 * q + -(-nblk // 2))
                if q == EARLY:
                    dve.wait_ge(s_bb, EARLY)
                v = b_st[:, q % 4, 0:nblk, :]
                nc.vector.tensor_tensor(v, v, bc[:].unsqueeze(1).to_broadcast([P, nblk, D]), ALU.add).then_inc(s_bb, 1)

            def positions(g, k, u):
                dve.wait_ge(rank_mm, g + 1)
                if not zeroth(g):
                    dve.wait_ge(pos_ready, g)
                nc.vector.tensor_tensor(prod[:], bank[1][:, 0:BK * NG_COLS].rearrange("p (b j) -> p b j", j=NG_COLS),
                                        onehot[:, :, bass.ds(g * NG_COLS, NG_COLS)], ALU.mult).then_inc(rank_read, 1)
                dve.wait_ge(rank_read, g + 1)
                if not below(g, 0, RING):
                    dve.wait_ge(st_free[k], u * 16 * NG_COLS)
                with nc.allow_low_precision(reason="integers below 2**24"):
                    nc.vector.tensor_reduce(pos_idx[:, k, :], prod[:].rearrange("p b j -> p j b"), AX.X, ALU.add).then_inc(pos_ready, 1)

            with dve.If_eq(groups_without_window(dve), 0):
                def step(g, k, u):
                    for h in range(2):
                        if not zeroth(g):
                            dve.wait_ge(hd_t, 2 * g + h - 1)
                        nc.vector.tensor_tensor(hot_d[:, h, :, :], iota_row[:].unsqueeze(1).to_broadcast([P, 4, P]),
                                                dst_rel[:, bass.ds(g * NG_COLS + 4 * h, 4)].unsqueeze(2).to_broadcast([P, 4, P]),
                                                ALU.is_equal).then_inc(hd_made, 1)
                    positions(g, k, u)
                group_trips(dve, step)
            with dve.Else():
                def step(g, k, u):
                    positions(g, k, u)
                    if not (isinstance(g, int) and g + 2 >= NG):
                        kk = (k + 2) % RING
                        if not below(g, 2, RING):
                            dve.wait_ge(b_ready[kk], (u + (k + 2) // RING) * 16 * NG_COLS)
                        nc.vector.tensor_copy(dst_idx[:, kk, :], dst_i[:, bass.ds((g + 2) * NG_COLS, NG_COLS)]).then_inc(dsti_ready, 1)
                    dve.wait_ge(b_ready[k], (u + 1) * 16 * NG_COLS)
                    for h in range(2):
                        dve.wait_ge(h_done, 2 * g + h + 1)
                        nc.vector.tensor_tensor(stage[:, k, 4 * h:4 * h + 4, 0:D],
                                                bank[6 + h][:].rearrange("p (t d) -> p t d", t=4),
                                                b_rows[:, k, 4 * h:4 * h + 4, :], ALU.add).then_inc(st_ready, 1)
                group_trips(dve, step)

            def step(n, k, i, on):
                def select():
                    s, kk = n + 2, (k + 2) % NODE_RING
                    dve.wait_ge(hs_ready[kk], (i + (k + 2) // NODE_RING) * 16 + 16)
                    if not below(n, 2, NODE_RING):
                        dve.wait_ge(n_o, s - NODE_RING + 1)
                    nc.vector.tensor_tensor(sel[kk][:, 0:DVE_J, :], iota_row[:].unsqueeze(1).to_broadcast([P, DVE_J, P]),
                                            hs[kk][:, 0:DVE_J, D:ROW].to_broadcast([P, DVE_J, P]), ALU.is_equal).then_inc(n_sel, 1)
                if on(0):
                    s, b2 = n, k % 2
                    dve.wait_ge(n_a, s + 1)
                    if not below(n, 0, 2):
                        dve.wait_ge(n_ssq, s - 1)
                        dve.wait_ge(n_scaled, s - 1)
                    nc.vector.tensor_tensor(pre[b2], bank[2 + b2][:].rearrange("p (j d) -> p j d", j=SJ),
                                            hs[k][:, :, 0:D], ALU.add).then_inc(n_pre, 1)
                if on(-1):
                    s, b2, kk = n - 1, (k + 1) % 2, (k - 1) % NODE_RING
                    dve.wait_ge(n_std, s + 1)
                    nc.vector.reciprocal(rstd[:, b2, :], std[:, b2, :]).then_inc(n_rs, 1)
                    dve.wait_ge(n_rs, s + 1)
                    dve.wait_ge(n_scaled, s + 1)
                    for j in range(SJ):
                        if j == SEL_AT and on(2):
                            select()
                        a = nc.vector.scalar_tensor_tensor(msg[kk][:, j, 0:D], msg[kk][:, j, 0:D], rstd[:, b2, j:j + 1],
                                                           neg_beta[:], ALU.mult, ALU.max)
                    a.then_inc(n_msg, 1)
                elif on(2):
                    select()
                if on(-3):
                    s, b2 = n - 3, (k - 3) % 2
                    at = dve.value_load(blk_i[0:1, bass.ds(s, 1)], min_val=0, max_val=NB - 1)
                    dve.wait_ge(n_o, s + 1)
                    if below(n, -3, 1):
                        dve.wait_ge(y_head, 16)
                    else:
                        dve.wait_ge(n_run, s)
                    if not isinstance(n, int) and k == 0:
                        dve.wait_ge(y_rest, 16 * (NODE_RING - 1) + 1)
                    yb = sums[:, bass.ds(at, 1), :].squeeze(1)
                    nc.vector.tensor_tensor(yb, yb, bank[4 + (k - 3) % 3][:, 0:ROW], ALU.add).then_inc(n_run, 1)
            for k in range(RING):
                dve.wait_ge(st_free[k], 16 * NG_COLS * (NIT + (k < LAST)))
            nc.vector.memset(msg_room[:, :, :, D:ROW], 1.0).then_inc(n_cnt, 1)
            nc.vector.memset(sums[:, :, D:ROW], 0.0).then_inc(n_cnt, 1)
            nc.vector.tensor_copy(y[:, NB - 1, :], x_last[:]).then_inc(y_rest, 1)
            dve.wait_ge(n_cnt, 2)
            n_trips = trip_count(dve)
            super_trips(dve, n_trips, step)

            for c in range(NCH + 1):
                if c < NCH:
                    dve.wait_ge(f_add, c + 1)
                    for t in range(c * CH, (c + 1) * CH):
                        a = nc.vector.bn_stats(ystat[:, t, :], y[:, t, :])
                    a.then_inc(f_st, 1)
                    dve.wait_ge(f_st, c + 1)
                    for t in range(c * CH, (c + 1) * CH):
                        a = nc.vector.bn_aggr(ymv[:, t, :], ystat[:, t, :])
                    a.then_inc(f_mv, 1)
                if c > 0:
                    lo, hi = (c - 1) * CH, c * CH
                    dve.wait_ge(f_sd, c)
                    link(nc.vector.reciprocal(yrstd[:, lo:hi], ystd[:, lo:hi]))
                    nc.vector.scalar_tensor_tensor(yshift[:, lo:hi], ymv[:, lo:hi, 0], -1.0, yrstd[:, lo:hi],
                                                   ALU.mult, ALU.mult).then_inc(f_sc, 1)
                    if c - 1 not in ACT_CHUNKS:
                        for t in range(lo, hi):
                            a = nc.vector.tensor_scalar(y2[:, t, :], y[:, t, :], ymv[:, t, 0:1], yrstd[:, t:t + 1],
                                                        ALU.subtract, ALU.mult)
                        a.then_inc(f_yd, 1)


_INS = ['x', 'src', 'dst', 'edge_attr_128', 'L0_gnn_W', 'L0_gnn_b', 'L0_gnn_gamma', 'L0_gnn_beta']
_OUTS = [((6250, 128), 'float32')]


def kernel(**inputs):
    import numpy as _np
    import concourse.bacc as _bacc
    from concourse import mybir as _mybir
    from concourse.bass_utils import run_bass_kernel_spmd as _run

    nc = _bacc.Bacc("TRN2", target_bir_lowering=False, num_devices=1)
    arrays, args = {}, []
    for name in _INS:
        a = _np.ascontiguousarray(inputs[name])
        arrays[f"in_{name}_dram"] = a
        args.append(nc.dram_tensor(f"in_{name}_dram", a.shape, _mybir.dt.from_np(a.dtype), kind="ExternalInput").ap())
    for i, (shape, dtype) in enumerate(_OUTS):
        dt = _mybir.dt.from_np(_np.dtype(dtype))
        args.append(nc.dram_tensor(f"out_{i}_dram", shape, dt, kind="ExternalOutput").ap())
    bass_gnn_resnorm(nc, *args)
    r = _run(nc, [arrays], core_ids=[0])
    got = tuple(r.results[0][f"out_{i}_dram"] for i in range(len(_OUTS)))
    return got[0]
```
